# Optimizing a Trainium2 kernel written in Bass

```python
import numpy as np
import jax
import jax.numpy as jnp

def _softmax(x, axis=-1):
    return jax.nn.softmax(x, axis=axis)

def _gelu(x):
    return jax.nn.gelu(x, approximate=True)

def _silu(x):
    return jax.nn.silu(x)

def _sigmoid(x):
    return jax.nn.sigmoid(x)

def _layernorm(x, axis=-1, eps=1e-05):
    m = jnp.mean(x, axis=axis, keepdims=True)
    v = jnp.var(x, axis=axis, keepdims=True)
    return (x - m) / jnp.sqrt(v + eps)

def _scatter_add(tgt, idx, src, axis=0):
    return tgt.at[idx].add(src)

def _segment_sum(src, seg, n):
    return jax.ops.segment_sum(src, seg, n)
kernel_name = 'mk_adj_preln_d4_adj_r2_6d8cc0'

def setup_inputs(seed: int=0):
    np.random.seed(seed)
    _w = jnp.asarray

    def _rec_inputs():
        import jax
        import jax.numpy as jnp
        _gk = jax.random.key(seed)
        x = -0.0005207 + 1.001 * jax.random.normal(jax.random.fold_in(_gk, 1), (64, 128, 64), jnp.float32)
        _a = jax.random.bernoulli(jax.random.fold_in(_gk, 2), 0.125, (64, 128, 128))
        _a = jnp.logical_or(_a, jnp.eye(128, dtype=bool))
        _af = _a.astype(jnp.float32)
        _af = _af * jax.random.uniform(jax.random.fold_in(_gk, 3), (64, 128, 128), jnp.float32, 0.05, 1)
        adj = _af
        return (x, adj)
    x, adj = _rec_inputs()

    def _L0_gnn_setup():
        import jax, jax.numpy as jnp
        import numpy as np
        key = jax.random.key(seed)
        k1, k2 = jax.random.split(key)
        B, N, D = (8, 2048, 64)
        x = jax.random.normal(k1, (B, N, D), dtype=jnp.float32)
        A = jax.random.uniform(k2, (B, N, N), dtype=jnp.float32)
        return {'x': x, 'A': A}
    _L0_gnn_all = _L0_gnn_setup()
    _L0_gnn_in = {k: v for k, v in _L0_gnn_all.items() if k in ()}
    del _L0_gnn_all

    def _L1_gnn_setup():
        import jax, jax.numpy as jnp
        import numpy as np
        key = jax.random.key(seed)
        ks = jax.random.split(key, 6)
        B, N, F, H, O = (2, 256, 64, 192, 64)
        x = jax.random.normal(ks[0], (B, N, F), dtype=jnp.float32)
        adj = jax.random.normal(ks[1], (B, N, N), dtype=jnp.float32)
        W1 = jax.random.normal(ks[2], (2 * F, H), dtype=jnp.float32) * (1.0 / np.sqrt(2 * F))
        b1 = jax.random.normal(ks[3], (H,), dtype=jnp.float32) * 0.02
        W2 = jax.random.normal(ks[4], (H, O), dtype=jnp.float32) * (1.0 / np.sqrt(H))
        b2 = jax.random.normal(ks[5], (O,), dtype=jnp.float32) * 0.02
        return {'x': x, 'adj': adj, 'W1': W1, 'b1': b1, 'W2': W2, 'b2': b2}
    _L1_gnn_all = _L1_gnn_setup()
    _L1_gnn_in = {k: v for k, v in _L1_gnn_all.items() if k in ('W1', 'b1', 'W2', 'b2')}
    del _L1_gnn_all

    def _L2_gnn_setup():
        import jax, jax.numpy as jnp
        import numpy as np
        B, L, C, OUT = (32, 512, 64, 64)
        BN_EPS = 1e-05
        key = jax.random.key(seed)
        kH, kA, kW = jax.random.split(key, 3)
        H = jax.random.normal(kH, (B, L, C), dtype=jnp.float32)
        A = jax.random.uniform(kA, (B, L, L), dtype=jnp.float32)
        gamma = jnp.ones((C,), jnp.float32)
        beta = jnp.zeros((C,), jnp.float32)
        W = jax.random.normal(kW, (C, OUT), dtype=jnp.float32) * 0.05
        b = jnp.zeros((OUT,), jnp.float32)
        return {'H': H, 'A': A, 'gamma': gamma, 'beta': beta, 'W': W, 'b': b}
    _L2_gnn_all = _L2_gnn_setup()
    _L2_gnn_in = {k: v for k, v in _L2_gnn_all.items() if k in ('gamma', 'beta', 'W', 'b')}
    del _L2_gnn_all

    def _L3_gnn_setup():
        import jax, jax.numpy as jnp
        import numpy as np
        ALPHA = 0.2
        NEG_INF = -9000000000000000.0
        key = jax.random.key(seed)
        k1, k2, k3, k4 = jax.random.split(key, 4)
        B, N, F_in, F_out = (32, 512, 64, 64)
        h = jax.random.normal(k1, (B, N, F_in), dtype=jnp.float32)
        adj = (jax.random.uniform(k2, (B, N, N)) < 0.05).astype(jnp.float32)
        adj = jnp.maximum(adj, jnp.eye(N, dtype=jnp.float32)[None])
        W = jax.random.normal(k3, (F_in, F_out), dtype=jnp.float32) * 0.1
        a = jax.random.normal(k4, (2 * F_out, 1), dtype=jnp.float32) * 0.1
        return {'h': h, 'adj': adj, 'W': W, 'a': a}
    _L3_gnn_all = _L3_gnn_setup()
    _L3_gnn_in = {k: v for k, v in _L3_gnn_all.items() if k in ('W', 'a')}
    del _L3_gnn_all
    return {'x': x, 'adj': adj, 'L1_gnn_W1': _L1_gnn_in['W1'], 'L1_gnn_b1': _L1_gnn_in['b1'], 'L1_gnn_W2': _L1_gnn_in['W2'], 'L1_gnn_b2': _L1_gnn_in['b2'], 'L2_gnn_gamma': _L2_gnn_in['gamma'], 'L2_gnn_beta': _L2_gnn_in['beta'], 'L2_gnn_W': _L2_gnn_in['W'], 'L2_gnn_b': _L2_gnn_in['b'], 'L3_gnn_W': _L3_gnn_in['W'], 'L3_gnn_a': _L3_gnn_in['a']}

def reference(x, adj, L1_gnn_W1, L1_gnn_b1, L1_gnn_W2, L1_gnn_b2, L2_gnn_gamma, L2_gnn_beta, L2_gnn_W, L2_gnn_b, L3_gnn_W, L3_gnn_a):
    import jax
    import jax.numpy as jnp

    def _L0_gnn_ref(x, A):
        import jax, jax.numpy as jnp
        import numpy as np
        deg = jnp.clip(jnp.sum(A, axis=2, keepdims=True), 1.0, None)
        A_norm = A / deg
        messages = jnp.matmul(A_norm, x)
        return messages

    def _L1_gnn_ref(x, adj, W1, b1, W2, b2):
        import jax, jax.numpy as jnp
        import numpy as np
        F = x.shape[-1]
        mask = (adj > 0.0).astype(x.dtype)
        W1a, W1b = (W1[:F], W1[F:])
        xj_proj = x @ W1a
        diff = x[:, :, None, :] - x[:, None, :, :]
        h = jax.nn.relu(xj_proj[:, :, None, :] + diff @ W1b + b1)
        hm = jnp.einsum('bjkh,bjk->bjh', h, mask)
        deg = jnp.sum(mask, axis=-1)
        return hm @ W2 + deg[..., None] * b2

    def _L2_gnn_ref(H, A, gamma, beta, W, b):
        import jax, jax.numpy as jnp
        import numpy as np
        B, L, C, OUT = (32, 512, 64, 64)
        BN_EPS = 1e-05
        batch, l, c = H.shape
        Hf = H.reshape(batch * l, c)
        mean = Hf.mean(axis=0)
        var = jnp.mean((Hf - mean) ** 2, axis=0)
        Hn = ((Hf - mean) * jax.lax.rsqrt(var + BN_EPS) * gamma + beta).reshape(batch, l, c)
        d = A.sum(axis=2)
        A_norm = jnp.sqrt(d)[:, :, None] * A * jax.lax.rsqrt(d)[:, None, :]
        A_hat = jnp.eye(l, dtype=A.dtype) - A_norm
        X = Hn @ W + b
        out = jnp.einsum('bij,bjo->bio', A_hat, X)
        return jax.nn.leaky_relu(out, negative_slope=0.01)

    def _L3_gnn_ref(h, adj, W, a):
        import jax, jax.numpy as jnp
        import numpy as np
        ALPHA = 0.2
        NEG_INF = -9000000000000000.0
        F_out = W.shape[1]
        Wh = jnp.matmul(h, W)
        a1, a2 = (a[:F_out, 0], a[F_out:, 0])
        s1 = Wh @ a1
        s2 = Wh @ a2
        e = s1[:, :, None] + s2[:, None, :]
        e = jnp.where(e > 0, e, ALPHA * e)
        attn_logits = jnp.where(adj > 0, e, NEG_INF)
        attention = jax.nn.softmax(attn_logits, axis=-1)
        h_out = jnp.matmul(attention, Wh)
        return jax.nn.elu(h_out)
    h = jnp.maximum(_layernorm(x, axis=-1), 0.0)
    x = x + _L0_gnn_ref(h, adj)
    h = jnp.maximum(_layernorm(x, axis=-1), 0.0)
    x = x + _L1_gnn_ref(h, adj, L1_gnn_W1, L1_gnn_b1, L1_gnn_W2, L1_gnn_b2)
    h = jnp.maximum(_layernorm(x, axis=-1), 0.0)
    x = x + _L2_gnn_ref(h, adj, L2_gnn_gamma, L2_gnn_beta, L2_gnn_W, L2_gnn_b)
    h = jnp.maximum(_layernorm(x, axis=-1), 0.0)
    x = x + _L3_gnn_ref(h, adj, L3_gnn_W, L3_gnn_a)
    return x

_drawn_inputs = setup_inputs


def setup_inputs(seed=0):
    import zlib

    import numpy as np

    out = dict(_drawn_inputs(seed))
    spreads = {'L2_gnn_gamma': (1.0, 0.6), 'L2_gnn_beta': (0.0, 0.1), 'L2_gnn_b': (0.0, 0.1)}
    factors = {'L3_gnn_a': 34.724}
    for name, (base, spread) in spreads.items():
        noise = np.random.default_rng([zlib.crc32(name.encode()), seed]).standard_normal(out[name].shape)
        drawn = base * np.exp(spread * noise) if base else spread * noise
        out[name] = jnp.asarray(drawn.astype(out[name].dtype))
    for name, factor in factors.items():
        out[name] = (out[name] * factor).astype(out[name].dtype)
    return out
```

```python
from contextlib import ExitStack

import concourse.bass as bass
from concourse import mybir

F32 = mybir.dt.float32
BF16 = mybir.dt.bfloat16
ALU = mybir.AluOpType
ACT = mybir.ActivationFunctionType
AX_X = mybir.AxisListType.X

B, N, D, H = 64, 128, 64, 192
GB = 4
NG = B // GB
HALF = H // 2
HB = 4
QB = HALF // HB
OH = 32
NOH = HALF // OH
KZ = 3 * OH + 3
LAG = 3
LN_EPS = 1e-5
BN_EPS = 1e-5
BIG = 2.0 ** 100
NEG_INF = -9000000000000000.0
LEAK2, LEAK3 = 0.01, 0.2


def layers(nc, x_d, adj_d, w1_d, b1_d, w2_d, b2_d, gamma_d, beta_d, w3_d, b3_d, w4_d, a_d, out_d):
    with ExitStack() as ctx:
        def sb(name, shape, dt=F32):
            return ctx.enter_context(nc.sbuf_tensor(name, shape, dt))

        def sem(name):
            return ctx.enter_context(nc.semaphore(name))

        bank = [ctx.enter_context(nc.psum_tensor(f"bank{i}", [128, 512], F32)) for i in range(8)]

        ident = sb("ident", [N, N])
        negbig_ident = sb("negbig_ident", [N, N], BF16)
        ones_bf = sb("ones_bf", [N, N], BF16)
        ones_f = sb("ones_f", [N, N])
        w1a = sb("w1a", [D, H])
        w1b = sb("w1b", [D, H])
        w_t = sb("w_t", [D + 1, 2, 2, HALF])
        w_j = sb("w_j", [D + 1, 2, 2, HALF])
        w2 = sb("w2", [HALF, 2, D])
        b2_bc = sb("b2_bc", [N, D])
        gamma_c = sb("gamma_c", [D, 1])
        beta_c = sb("beta_c", [D, 1])
        w3 = sb("w3", [D, D])
        b3_bc = sb("b3_bc", [N, D])
        w4 = sb("w4", [D, D])
        w4_t = sb("w4_t", [D, D])
        a_c = sb("a_c", [D, 2])
        wa_bc = sb("wa_bc", [D, 2, N])
        x_all = sb("x_all", [N, B + 1, D])
        h_t_all = sb("h_t_all", [D + 1, B + 1, N])
        h2_all = sb("h2_all", [N, B, D])
        edge_t_all = sb("edge_t_all", [N, B, N], BF16)
        no_edge_t_all = sb("no_edge_t_all", [N, B, N], BF16)
        abuf = [sb(f"abuf{u}", [N, GB, N]) for u in range(2)]
        a_t = sb("a_t", [N, GB, N])
        xc = sb("xc", [N, GB, D])
        sq = sb("sq", [N, GB, D])
        hn = sb("hn", [N, GB, D])
        tmp = sb("tmp", [N, GB, D])
        pairs = sb("pairs", [N, GB, N])
        pairs2 = sb("pairs2", [N, GB, N])
        stat = sb("stat", [N, 16, GB])
        rhs = [sb(f"rhs{i}", [KZ, HALF, N], BF16) for i in range(2)]
        lq = [sb(f"lq{i}", [KZ, NOH, N], BF16) for i in range(2)]
        f4 = [sb(f"f4_{i}", [N, HALF, 4], BF16) for i in range(2)]
        parts = sb("parts", [HALF, 3, 2, N], BF16)
        rest_t = sb("rest_t", [HALF, 2, N])
        rest_j = sb("rest_j", [N, HALF])
        h_t = sb("h_t", [D + 1, N])
        p_j = [sb(f"p_j{i}", [N, HALF]) for i in range(2)]
        g = [sb(f"g{i}", [N, HB, N], BF16) for i in range(8)]
        count_p = sb("count_p", [N, HALF])
        sum_q = sb("sum_q", [N, HALF])
        hm = sb("hm", [N, 2, HALF])
        hm_t = sb("hm_t", [HALF, 2, N])
        wait_carrier = sb("wait_carrier", [N, 1])
        bn_part = sb("bn_part", [N, D])
        bn_mean_bc = sb("bn_mean_bc", [N, D])
        bn_mean_c = sb("bn_mean_c", [D, 1])
        bn_v = sb("bn_v", [D, 8])
        ws3 = sb("ws3", [D, D])
        beta_bc = sb("beta_bc", [D, N])
        cb3 = sb("cb3", [N, D])
        d_t = sb("d_t", [D, GB, N])
        xl = sb("xl", [N, GB, D])
        yl = sb("yl", [N, GB, D])
        wh = sb("wh", [N, GB, D])
        pt = sb("pt", [N, GB, N])
        outb = [sb(f"outb{u}", [N, GB, D]) for u in range(2)]

        s_w = sem("weights_loaded")
        s_x = sem("x_loaded")
        s_a = [sem(f"adj_loaded{u}") for u in range(2)]
        s_const = sem("constants_made")
        s_pool = sem("pool_steps")
        s_wprep = sem("weights_prepared")
        s_dve = sem("vector_steps")
        names = ("a_used", "sqrt_in", "sqrt_out", "at_psum", "at_copied", "at_free", "h0_ready", "l0_psum", "h1_ready",
                 "h1t_psum", "h1t_copied", "mask_done")
        A = {n: sem("p0_" + n) for n in names}
        s_p0 = sem("phase0_done")
        s_zd = sem("z_for_vector")
        s_za = sem("z_for_scalar")
        s_gd = sem("g_from_vector")
        s_ga = sem("g_from_scalar")
        s_r = [sem(f"sums_ready{i}") for i in range(2)]
        s_comb = [sem(f"sums_combined{i}") for i in range(2)]
        s_ht = sem("h_t_copied")
        s_ptq = sem("pq_t_psum")
        s_pqj = sem("pq_j_psum")
        s_s1 = sem("first_parts")
        s_pj = sem("p_j_copied")
        s_rest = sem("rests_ready")
        s_p23 = sem("parts_ready")
        s_f23 = sem("f_parts_ready")
        s_fed = sem("z_operands_loaded")
        s_hmt = sem("hm_t_psum")
        s_hmc = sem("hm_t_copied")
        s_y = sem("edge_out_psum")
        s_x2 = sem("x2_ready")
        s_edge0 = sem("edge_phase_prepared")
        s_bn = sem("bn_vector")
        s_bnp = sem("bn_psum")
        s_bna = sem("bn_scalar")
        names = ("a_used", "sqrt_in", "sqrt_out", "at_psum", "at_copied", "dt_psum", "dt_copied", "x_psum",
                 "y_ready", "ay_psum", "h3_ready", "h3t_psum", "h3t_copied", "e_psum", "wh_psum", "wh_copied", "leaky",
                 "max_ready", "exp_done", "pt_psum", "pt_copied", "att_psum", "att_scaled", "elu_exp", "out_ready",
                 "dt_used")
        L = {n: sem("p2_" + n) for n in names}
        s_out = [sem(f"out_stored{u}") for u in range(2)]
        s_a2 = [sem(f"adj_loaded_again{u}") for u in range(2)]

        block = ctx.enter_context(nc.Block())

        def own_steps(eng, s, start, per_round=0, rnd=0):
            done = [0]

            def step(ins):
                done[0] += 1
                ins.then_inc(s, 1)
                eng.wait_ge(s, start + per_round * rnd + done[0])
            step.done = done
            return step

        adj_v = adj_d.rearrange("(g b) i k -> g i b k", b=GB)
        out_v = out_d.rearrange("(g b) j f -> g j b f", b=GB)

        V_LN = 10
        V_P0 = 2 * V_LN + 10

        V_P2 = V_LN + 17


        @block.sync
        def _(sp):
            x_v = x_d.rearrange("b j f -> j b f")
            for c in range(4):
                nb = B // 4
                sp.dma_start(x_all[:, 1 + c * nb:1 + (c + 1) * nb, :], x_v[:, c * nb:(c + 1) * nb, :]).then_inc(s_x, 16)
                if c == 0:
                    for u in range(2):
                        sp.dma_start(abuf[u][:], adj_v[u]).then_inc(s_a[u], 16)
            with sp.Fori(0, NG // 2 - 1) as t:
                for u in range(2):
                    sp.wait_ge(A["a_used"], t * 2 + u + 1)
                    sp.dma_start(abuf[u][:], adj_v[bass.ds(t * 2 + u + 2, 1)].rearrange("o i b k -> (o i) b k")).then_inc(s_a[u], 16)

            def feed(m, half):
                sp.wait_ge(s_p23, m + 1)
                for c in range(3):
                    sp.dma_start(rhs[half][3 * OH + c:3 * OH + c + 1, :, :], parts[:, c, 0, :]).then_inc(s_fed, 16)
                    for n in range(NOH):
                        sp.dma_start(lq[half][OH * c:OH * (c + 1), n, :],
                                     parts[OH * n:OH * (n + 1), c, 1, :]).then_inc(s_fed, 16)

            sp.wait_ge(s_const, 1)
            feed(0, 0)
            with sp.Fori(0, B) as b:
                feed(b * 2 + 1, 1)
                feed(b * 2 + 2, 0)

            for u in range(2):
                sp.wait_ge(A["a_used"], NG)
                sp.dma_start(abuf[u][:], adj_v[u]).then_inc(s_a2[u], 16)
            def store(gi, u):
                sp.wait_ge(L["out_ready"], gi + 1)
                sp.dma_start(out_v[bass.ds(gi, 1)].rearrange("o j b f -> (o j) b f"), outb[u][:]).then_inc(s_out[u], 16)

            with sp.Fori(0, NG // 2 - 1) as t:
                for u in range(2):
                    gi = t * 2 + u
                    sp.wait_ge(L["a_used"], gi + 1)
                    sp.dma_start(abuf[u][:], adj_v[bass.ds(gi + 2, 1)].rearrange("o i b k -> (o i) b k")).then_inc(s_a2[u], 16)
                    store(gi, u)
            for u in range(2):
                store(NG - 2 + u, u)
            for u in range(2):
                sp.wait_ge(s_out[u], 16 * (NG // 2))

        @block.gpsimd
        def _(pool):
            step = own_steps(pool, s_pool, 0)
            gp = nc.gpsimd
            small = [(w1a[:], w1_d[0:D, :]), (w1b[:], w1_d[D:2 * D, :]),
                     (w_t[D:D + 1, :, 0, :], b1_d.rearrange("(o c h) -> o c h", o=1, c=2)),
                     (w_j[D:D + 1, :, 0, :], b1_d.rearrange("(o c h) -> o c h", o=1, c=2)),
                     (w2[:], w2_d.rearrange("(c h) o -> h c o", c=2)),
                     (b2_bc[:], b2_d.rearrange("(o f) -> o f", o=1).broadcast_to([N, D])),
                     (gamma_c[:], gamma_d.rearrange("(f o) -> f o", o=1)),
                     (beta_c[:], beta_d.rearrange("(f o) -> f o", o=1)),
                     (w3[:], w3_d), (b3_bc[:], b3_d.rearrange("(o f) -> o f", o=1).broadcast_to([N, D])),
                     (w4[:], w4_d), (a_c[:, 0:1], a_d[0:D, :]), (a_c[:, 1:2], a_d[D:2 * D, :])]
            for dst, src in small:
                pool.dma_start(dst, src).then_inc(s_w, 16)
            step(gp.memset(ident[:], 0.0))
            step(gp.affine_select(out=ident[:], in_=ident[:], compare_op=ALU.not_equal, fill=1.0, base=0,
                                  pattern=[[-1, N]], channel_multiplier=1))
            step(gp.memset(negbig_ident[:], 0.0))
            step(gp.affine_select(out=negbig_ident[:], in_=negbig_ident[:], compare_op=ALU.not_equal, fill=-BIG, base=0,
                                  pattern=[[-1, N]], channel_multiplier=1))
            step(gp.memset(ones_bf[:], 1.0))
            for i in range(2):
                step(gp.memset(rhs[i][:], 0.0))
                for c in range(3):
                    v = rhs[i][OH * c:OH * (c + 1)].rearrange("p (n h) j -> p n h j", h=OH)
                    step(gp.affine_select(out=v, in_=v, compare_op=ALU.not_equal, fill=1.0, base=0,
                                          pattern=[[0, NOH], [-1, OH], [0, N]], channel_multiplier=1))
                step(gp.memset(lq[i][3 * OH:KZ], 1.0))
            gp.memset(ones_f[:], 1.0).then_inc(s_const, 1)

            def later_parts(m):
                half = m[1]
                n = m[0]
                pool.wait_ge(s_rest, n + 1)
                gp.tensor_tensor(wait_carrier[:], ones_f[:, 0:1], ones_f[:, 0:1], ALU.mult)
                gp.tensor_copy(parts[:, 1], rest_t[:]).then_inc(s_pool, 1)
                gp.tensor_copy(f4[half][:, :, 2], rest_j[:]).then_inc(s_pool, 1)
                pool.wait_ge(s_pool, pool_base + n * 2 + 2)
                gp.tensor_tensor(parts[:, 2], rest_t[:], parts[:, 1], ALU.subtract).then_inc(s_p23, 1)
                gp.tensor_tensor(f4[half][:, :, 3], rest_j[:], f4[half][:, :, 2], ALU.subtract).then_inc(s_f23, 1)

            pool.wait_ge(s_const, 1)
            pool_base = step.done[0]
            later_parts((0, 0))
            with pool.Fori(0, B) as b:
                later_parts((b * 2 + 1, 1))
                later_parts((b * 2 + 2, 0))

        @block.scalar
        def _(act):
            sc = nc.scalar

            with act.Fori(0, NG // 2) as t:
                for u in range(2):
                    gi = t * 2 + u
                    act.wait_ge(A["at_psum"], gi + 1)
                    act.wait_ge(A["mask_done"], gi)
                    act.wait_ge(A["l0_psum"], gi)
                    sc.copy(a_t[:].rearrange("p b k -> p (b k)"), bank[0][:]).then_inc(A["at_copied"], 1)
                    for k in range(2):
                        act.wait_ge(A["sqrt_in"], gi * 2 + k + 1)
                        sc.activation(stat[:, 3, :], stat[:, 2, :], ACT.Sqrt).then_inc(A["sqrt_out"], 1)
                    act.wait_ge(A["h1t_psum"], gi + 1)
                    sc.copy(h_t_all[0:D, bass.ds(gi * GB, GB), :],
                            bank[2][0:D, :].rearrange("p (b k) -> p b k", b=GB)).then_inc(A["h1t_copied"], 1)

            def copy_h_t(m, gb):
                act.wait_ge(s_ptq, m)
                act.wait_ge(s_pqj, m)
                sc.copy(h_t[:], h_t_all[:, gb, :]).then_inc(s_ht, 1)

            def first_parts(m, half, combined):
                act.wait_ge(s_ptq, m + 1)
                act.wait_ge(s_fed, 16 * 12 * m)
                sc.copy(parts[:, 0].rearrange("p a b -> p (a b)"), bank[6][0:HALF, 0:2 * N]).then_inc(s_s1, 1)
                act.wait_ge(s_pqj, m + 1)
                act.wait_ge(s_f23, m)
                sc.copy(f4[half][:, :, 1], bank[7][:, HALF:2 * HALF]).then_inc(s_s1, 1)
                act.wait_ge(s_comb[half], combined)
                sc.copy(p_j[half][:], bank[7][:, 0:HALF]).then_inc(s_pj, 1)

            act.wait_ge(s_p0, 2)
            act.wait_ge(A["h1t_copied"], NG)
            copy_h_t(0, 0)
            first_parts(0, 0, 0)
            with act.Fori(0, B) as b:
                for half in range(2):
                    m = b * 2 + half + 1
                    for q in range(QB):
                        if q == 2:
                            copy_h_t(m, bass.ds(b + half, 1))
                        if q == 7:
                            first_parts(m, 1 - half, b + 1)
                        if q == 12 and half == 0:
                            act.wait_ge(s_hmt, b + 1)
                            act.wait_ge(s_y, b)
                            sc.copy(hm_t[:].rearrange("p c j -> p (c j)"), bank[6][0:HALF, 2 * N:4 * N]).then_inc(s_hmc, 1)
                        if q % 2:
                            n = half * QB + q
                            act.wait_ge(s_za, b * QB + n // 2 + 1)
                            sc.activation(g[n % 8][:].rearrange("p h j -> p (h j)"), bank[n % 4][:], ACT.Sign).then_inc(s_ga, 1)
            act.wait_ge(s_hmt, B + 1)
            act.wait_ge(s_y, B)
            sc.copy(hm_t[:].rearrange("p c j -> p (c j)"), bank[6][0:HALF, 2 * N:4 * N]).then_inc(s_hmc, 1)

            with act.Fori(0, NG) as gi:
                act.wait_ge(L["sqrt_in"], gi + 1)
                sc.activation(stat[:, 3, :], stat[:, 2, :], ACT.Sqrt).then_inc(L["sqrt_out"], 1)
            act.wait_ge(s_bn, 2)
            sc.copy(beta_bc[:], beta_c[:].broadcast_to([D, N])).then_inc(s_bna, 1)
            act.wait_ge(s_bn, 4)
            sc.activation(bn_v[:, 1:2], bn_v[:, 0:1], ACT.Sqrt).then_inc(s_bna, 1)

            with act.Fori(0, NG // 2) as t:
                for u in range(2):
                    gi = t * 2 + u
                    act.wait_ge(L["at_psum"], gi + 1)
                    act.wait_ge(L["ay_psum"], gi)
                    sc.copy(a_t[:].rearrange("p b k -> p (b k)"), bank[0][:]).then_inc(L["at_copied"], 1)
                    act.wait_ge(L["sqrt_in"], NG + gi * 2 + 1)
                    sc.activation(stat[:, 3, :], stat[:, 2, :], ACT.Sqrt).then_inc(L["sqrt_out"], 1)
                    act.wait_ge(L["sqrt_in"], NG + gi * 2 + 2)
                    sc.activation(stat[:, 3, :], stat[:, 2, :], ACT.Sqrt).then_inc(L["sqrt_out"], 1)
                    act.wait_ge(L["h3t_psum"], gi + 1)
                    sc.copy(d_t[:].rearrange("p b k -> p (b k)"), bank[2][0:D, :]).then_inc(L["h3t_copied"], 1)
                    act.wait_ge(L["wh_psum"], gi + 1)
                    act.wait_ge(L["att_psum"], gi)
                    sc.copy(wh[:].rearrange("p b k -> p (b k)"), bank[3][:, 0:GB * D]).then_inc(L["wh_copied"], 1)
                    act.wait_ge(L["e_psum"], gi + 1)
                    sc.copy(pairs[:].rearrange("p b k -> p (b k)"), bank[4][:]).then_inc(L["leaky"], 1)
                    act.wait_ge(L["max_ready"], gi + 1)
                    for i in range(GB):
                        last = sc.activation(pairs[:, i, :], pairs2[:, i, :], ACT.Exp, bias=stat[:, 9, i:i + 1],
                                             accum_out=stat[:, 10, i:i + 1])
                    last.then_inc(L["exp_done"], 1)
                    act.wait_ge(L["pt_psum"], gi + 1)
                    sc.copy(pt[:].rearrange("p b k -> p (b k)"), bank[5][:]).then_inc(L["pt_copied"], 1)
                    act.wait_ge(L["att_scaled"], gi + 1)
                    sc.activation(yl[:], tmp[:], ACT.Exp).then_inc(L["elu_exp"], 1)

        @block.tensor
        def _(pe):
            te = nc.tensor

            pe.wait_ge(s_const, 1)
            pe.wait_ge(s_w, 16 * 13)
            te.transpose(bank[0][0:D, 0:D], w4[:], ident[0:D, 0:D]).then_inc(s_bnp, 1)
            pe.wait_ge(s_wprep, 2)
            te.matmul(bank[0][0:D, 64:66], w4_t[:], a_c[:], start=True, stop=True).then_inc(s_bnp, 1)
            pe.wait_ge(s_wprep, 3)
            with pe.Fori(0, NG // 2) as t:
                for u in range(2):
                    gi = t * 2 + u
                    pe.wait_ge(s_a[u], t * 16 + 16)
                    pe.wait_ge(A["at_copied"], gi)
                    for i in range(GB):
                        last = te.transpose(bank[0][:, N * i:N * (i + 1)], abuf[u][:, i, :], ident[:])
                    last.then_inc(A["at_psum"], 1)
                    pe.wait_ge(A["at_copied"], gi + 1)
                    pe.wait_ge(A["h0_ready"], gi + 1)
                    for i in range(GB):
                        last = te.matmul(bank[1][:, D * i:D * (i + 1)], a_t[:, i, :], hn[:, i, :], start=True, stop=True)
                    last.then_inc(A["l0_psum"], 1)
                    pe.wait_ge(A["h1_ready"], gi + 1)
                    te.matmul(bank[2][:, 511:512], ident[:], ones_f[:, 0:1], start=True, stop=True)
                    for i in range(GB):
                        last = te.transpose(bank[2][0:D, N * i:N * (i + 1)], hn[:, i, :], ident[:])
                    last.then_inc(A["h1t_psum"], 1)

            def project(m, half):
                pe.wait_ge(s_ht, m + 1)
                pe.wait_ge(s_rest, m)
                pe.wait_ge(s_pj, m)
                for k in range(2):
                    last = te.matmul(bank[6][0:HALF, N * k:N * (k + 1)], w_t[:, half, k, :], h_t[:], start=True, stop=True)
                last.then_inc(s_ptq, 1)
                te.matmul(bank[7][:, 0:2 * HALF], h_t[:], w_j[:, half].rearrange("p a b -> p (a b)"),
                          start=True, stop=True).then_inc(s_pqj, 1)

            def edge_out_t(done, rests):
                pe.wait_ge(s_comb[1], done)
                pe.wait_ge(s_rest, rests)
                for k in range(2):
                    last = te.transpose(bank[6][0:HALF, 2 * N + N * k:2 * N + N * (k + 1)], hm[:, k, :], ident[:])
                last.then_inc(s_hmt, 1)

            def edge_out(done):
                pe.wait_ge(s_hmc, done)
                pe.wait_ge(s_x2, done - 1)
                for k in range(2):
                    last = te.matmul(bank[7][:, 2 * HALF:2 * HALF + D], hm_t[:, k, :], w2[:, k, :], start=(k == 0), stop=(k == 1))
                last.then_inc(s_y, 1)

            pe.wait_ge(s_edge0, 1)
            project(0, 0)
            with pe.Fori(0, B) as b:
                def masked_sum(n):
                    half, q = n // QB, n % QB
                    if q == 0:
                        pe.wait_ge(s_comb[half], b + half)
                        pe.wait_ge(s_f23, b * 2 + half + 1)
                        te.matmul(bank[4 + half][:, 0:4 * HALF].rearrange("p (a o c) -> p a o c", o=2, c=4 * HB)[:, :, 1, :],
                                  ones_bf[:],
                                  f4[half][:].rearrange("p (a o h) c -> p a o (h c)", o=2, h=HB)[:, :, 1, :],
                                  start=True, stop=True, skip_group_check=True)
                    if n % 2:
                        pe.wait_ge(s_ga, b * QB + n // 2 + 1)
                    else:
                        pe.wait_ge(s_gd, b * QB + n // 2 + 3)
                    for i in range(HB):
                        h = q * HB + i
                        last = te.matmul(bank[4 + half][:, 4 * h:4 * h + 4], g[n % 8][:, i, :], f4[half][:, h, :],
                                         start=False, stop=True, skip_group_check=True)
                    if q == QB - 1:
                        last.then_inc(s_r[half], 1)

                for n in range(2 * QB):
                    half, q = n // QB, n % QB
                    if q == 4:
                        if half:
                            pe.wait_ge(s_hmc, b + 1)
                            pe.wait_ge(s_x2, b + 1)
                        project(b * 2 + half + 1, 1 - half)
                    if n == 10:
                        edge_out_t(b + 1, b * 2 + 2)
                    if n == 14:
                        edge_out(b + 1)
                    if q == 0:
                        pe.wait_ge(s_fed, b * (2 * 16 * 12) + (half + 1) * 16 * 12)
                    if n % 2:
                        if n >= 4:
                            pe.wait_ge(s_ga, b * QB + n // 2 - 1)
                        elif n == 3:
                            pe.wait_ge(s_ga, b * QB)
                    else:
                        pe.wait_ge(s_gd, b * QB + n // 2 + 1)
                    last = te.matmul(bank[n % 4][:], lq[half][:, q * HB // OH, :],
                                     rhs[half][:, q * HB:(q + 1) * HB, :].rearrange("p h j -> p (h j)"),
                                     start=True, stop=not n % 2)
                    if n % 2:
                        te.matmul(bank[n % 4][:].rearrange("p (h j) -> p h j", h=HB), negbig_ident[:],
                                  no_edge_t_all[:, bass.ds(b, 1), :].broadcast_to([N, HB, N]),
                                  start=False, stop=True).then_inc(s_za, 1)
                    else:
                        last.then_inc(s_zd, 1)
                    if n >= LAG:
                        masked_sum(n - LAG)
                for n in range(2 * QB - LAG, 2 * QB):
                    masked_sum(n)
            edge_out_t(B + 1, 2 * B + 1)
            edge_out(B + 1)

            pe.wait_ge(s_bn, 1)
            te.matmul(bank[0][:, 0:D], ones_f[:], bn_part[:], start=True, stop=True)
            te.matmul(bank[0][0:D, 64:65], bn_part[:], ones_f[:, 0:1], start=True, stop=True).then_inc(s_bnp, 1)
            pe.wait_ge(s_bn, 3)
            te.matmul(bank[0][0:D, 64:65], bn_part[:], ones_f[:, 0:1], start=True, stop=True).then_inc(s_bnp, 1)
            pe.wait_ge(s_bna, 1)
            te.matmul(bank[1][:, 0:D], beta_bc[:], w3[:], start=True, stop=True).then_inc(s_bnp, 1)
            pe.wait_ge(s_bn, 5)

            with pe.Fori(0, NG // 2) as t:
                for u in range(2):
                    gi = t * 2 + u
                    pe.wait_ge(s_a2[u], t * 16 + 16)
                    for i in range(GB):
                        last = te.transpose(bank[0][:, N * i:N * (i + 1)], abuf[u][:, i, :], ident[:])
                    last.then_inc(L["at_psum"], 1)
                    pe.wait_ge(L["dt_used"], gi + 1)
                    te.matmul(bank[1][:, 511:512], ident[:], ones_f[:, 0:1], start=True, stop=True)
                    for i in range(GB):
                        last = te.transpose(bank[1][0:D, N * i:N * (i + 1)], hn[:, i, :], ident[:])
                    last.then_inc(L["dt_psum"], 1)
                    pe.wait_ge(L["dt_copied"], gi + 1)
                    for i in range(GB):
                        last = te.matmul(bank[6][:, D * i:D * (i + 1)], d_t[:, i, :], ws3[:], start=True, stop=True)
                    last.then_inc(L["x_psum"], 1)
                    pe.wait_ge(L["at_copied"], gi + 1)
                    pe.wait_ge(L["y_ready"], gi + 1)
                    for i in range(GB):
                        last = te.matmul(bank[7][:, D * i:D * (i + 1)], a_t[:, i, :], yl[:, i, :], start=True, stop=True)
                    last.then_inc(L["ay_psum"], 1)
                    pe.wait_ge(L["h3_ready"], gi + 1)
                    te.matmul(bank[2][:, 511:512], ident[:], ones_f[:, 0:1], start=True, stop=True)
                    for i in range(GB):
                        last = te.transpose(bank[2][0:D, N * i:N * (i + 1)], hn[:, i, :], ident[:])
                    last.then_inc(L["h3t_psum"], 1)
                    pe.wait_ge(L["h3t_copied"], gi + 1)
                    for i in range(GB):
                        last = te.matmul(bank[3][:, D * i:D * (i + 1)], d_t[:, i, :], w4[:], start=True, stop=True)
                    last.then_inc(L["wh_psum"], 1)
                    for i in range(GB):
                        te.matmul(bank[4][:, N * i:N * (i + 1)], d_t[:, i, :], wa_bc[:, 0, :], start=True, stop=False)
                        last = te.matmul(bank[4][:, N * i:N * (i + 1)], wa_bc[:, 1, :], d_t[:, i, :], start=False, stop=True)
                    last.then_inc(L["e_psum"], 1)
                    pe.wait_ge(L["exp_done"], gi + 1)
                    for i in range(GB):
                        last = te.transpose(bank[5][:, N * i:N * (i + 1)], pairs[:, i, :], ident[:])
                    last.then_inc(L["pt_psum"], 1)
                    pe.wait_ge(L["pt_copied"], gi + 1)
                    pe.wait_ge(L["wh_copied"], gi + 1)
                    for i in range(GB):
                        last = te.matmul(bank[6][:, D * i:D * (i + 1)], pt[:, i, :], wh[:, i, :], start=True, stop=True)
                    last.then_inc(L["att_psum"], 1)

        @block.vector
        def _(dve):
            ve = nc.vector

            def bc(col, n=D, m=GB):
                return col.rearrange("p (b o) -> p b o", o=1).broadcast_to([N, m, n])

            def inverse_root(step, v, root, r, t, u):
                step(ve.reciprocal(r, root))
                step(ve.tensor_tensor(t, r, r, ALU.mult))
                step(ve.tensor_tensor(u, t, v, ALU.mult))
                step(ve.tensor_scalar(t, u, -0.5, 1.5, ALU.mult, ALU.add))

            def norm_relu(step, x, out, s_in, s_res, count, s_done):
                ve.memset(stat[:, 14, :], 0.0)
                step(ve.tensor_reduce(stat[:, 0, :], x, AX_X, ALU.add))
                step(ve.tensor_scalar(stat[:, 1, :], stat[:, 0, :], 1.0 / D, None, ALU.mult))
                step(ve.tensor_tensor(xc[:], x, bc(stat[:, 1, :]), ALU.subtract))
                step(ve.tensor_tensor(sq[:], xc[:], xc[:], ALU.mult))
                step(ve.tensor_reduce(stat[:, 0, :], sq[:], AX_X, ALU.add))
                ve.tensor_scalar(stat[:, 2, :], stat[:, 0, :], 1.0 / D, LN_EPS, ALU.mult, ALU.add).then_inc(s_in, 1)
                dve.wait_ge(s_in, count + 1)
                dve.wait_ge(s_res, count + 1)
                inverse_root(step, stat[:, 2, :], stat[:, 3, :], stat[:, 4, :], stat[:, 5, :], stat[:, 6, :])
                step(ve.tensor_tensor(stat[:, 7, :], stat[:, 4, :], stat[:, 5, :], ALU.mult))
                last = ve.scalar_tensor_tensor(out=out, in0=xc[:], scalar=0.0, in1=bc(stat[:, 7, :]),
                                               op0=ALU.max, op1=ALU.mult)
                if s_done is not None:
                    last.then_inc(s_done, 1)
                return last

            step = own_steps(dve, s_dve, 0)
            dve.wait_ge(s_w, 16 * 13)
            wa = w1a[:].rearrange("p (c h) -> p c h", c=2)
            wb = w1b[:].rearrange("p (c h) -> p c h", c=2)
            ve.tensor_tensor(w_t[0:D, :, 0, :], wa, wb, ALU.add).then_inc(s_edge0, 1)
            ve.tensor_tensor(w_j[0:D, :, 0, :], wa, wb, ALU.add)
            ve.tensor_scalar(w_t[0:D, :, 1, :], wb, -1.0, None, ALU.mult)
            wbq = wb.rearrange("p c (a o h) -> p (c a) o h", o=2, h=HB)
            wjq = w_j[0:D, :, 1, :].rearrange("p c (a o h) -> p c a o h", o=2, h=HB)
            for c in range(2):
                for o in range(2):
                    ve.tensor_scalar(wjq[:, c, :, o, :], wbq[:, c * (QB // 2):(c + 1) * (QB // 2), o, :],
                                     -1.0 if o == 0 else -0.5, None, ALU.mult)
                fq = f4[c][:].rearrange("p (a o h) c -> p a o h c", o=2, h=HB)
                ve.memset(fq[:, :, 0, :, 0], 1.0)
                ve.memset(fq[:, :, 1, :, 0], 0.5)
                ve.memset(p_j[c][:], 0.0)
            ve.memset(w_t[D:D + 1, :, 1, :], 0.0)
            ve.memset(w_j[D:D + 1, :, 1, :], 0.0)
            ve.memset(h_t_all[D:D + 1, :, :], 1.0)
            ve.memset(h_t_all[0:D, B, :], 0.0)
            ve.memset(hm[:], 0.0)
            step(ve.memset(x_all[:, 0, :], 0.0))
            ve.memset(bank[5][:], 0.0).then_inc(s_wprep, 1)
            dve.wait_ge(s_bnp, 1)
            ve.tensor_copy(w4_t[:], bank[0][0:D, 0:D]).then_inc(s_wprep, 1)
            dve.wait_ge(s_bnp, 2)
            step(ve.tensor_copy(bn_v[:, 0:2], bank[0][0:D, 64:66]))
            for k in range(2):
                last = ve.tensor_copy(wa_bc[:, k, :], bn_v[:, k:k + 1].broadcast_to([D, N]))
            last.then_inc(s_wprep, 1)
            base = step.done[0]

            dve.wait_ge(s_x, 64)
            with dve.Fori(0, NG // 2) as t:
                per = [0]
                for u in range(2):
                    gi = t * 2 + u
                    step = own_steps(dve, s_dve, base + u * V_P0, 2 * V_P0, t)
                    x = x_all[:, bass.ds(gi * GB + 1, GB), :]
                    if u == 0:
                        dve.wait_ge(A["h1t_psum"], gi)
                    else:
                        dve.wait_ge(A["h1t_psum"], gi)
                    norm_relu(step, x, hn[:], A["sqrt_in"], A["sqrt_out"], gi * 2, A["h0_ready"])
                    dve.wait_ge(s_a[u], t * 16 + 16)
                    step(ve.tensor_reduce(stat[:, 8, :], abuf[u][:], AX_X, ALU.add))
                    step(ve.tensor_scalar(stat[:, 9, :], stat[:, 8, :], 1.0, None, ALU.max))
                    step(ve.reciprocal(stat[:, 10, :], stat[:, 9, :]))
                    step(ve.tensor_scalar(pairs[:], abuf[u][:], 0.0, None, ALU.is_gt))
                    step(ve.tensor_reduce(stat[:, 11, :], pairs[:], AX_X, ALU.add))
                    dve.wait_ge(A["at_copied"], gi + 1)
                    ve.tensor_scalar(edge_t_all[:, bass.ds(gi * GB, GB), :], a_t[:], 0.0, None, ALU.is_gt)
                    step(ve.tensor_scalar(no_edge_t_all[:, bass.ds(gi * GB, GB), :], a_t[:], 0.0, None, ALU.is_le))
                    dve.wait_ge(A["at_psum"], gi + 1)
                    ve.memset(stat[:, 12, :], 0.0).then_inc(A["a_used"], 1)
                    ve.memset(stat[:, 13, :], 0.0).then_inc(A["mask_done"], 1)
                    dve.wait_ge(A["l0_psum"], gi + 1)
                    step(ve.tensor_tensor(tmp[:], bank[1][:, 0:GB * D].rearrange("p (b f) -> p b f", b=GB),
                                          bc(stat[:, 10, :]), ALU.mult))
                    step(ve.tensor_tensor(x, x, tmp[:], ALU.add))
                    norm_relu(step, x, hn[:], A["sqrt_in"], A["sqrt_out"], gi * 2 + 1, A["h1_ready"])
                    step(ve.tensor_tensor(tmp[:], b2_bc[:].rearrange("p (o f) -> p o f", o=1).broadcast_to([N, GB, D]),
                                          bc(stat[:, 11, :]), ALU.mult))
                    step(ve.tensor_tensor(x, x, tmp[:], ALU.add))
                    assert step.done[0] == V_P0, step.done
            ve.memset(bank[4][:], 0.0).then_inc(s_p0, 1)
            ve.memset(stat[:, 12, :], 0.0).then_inc(s_p0, 1)
            ve.memset(stat[:, 13, :], 0.0).then_inc(s_gd, 2)
            base = base + NG * V_P0

            def rests(m, half):
                dve.wait_ge(s_s1, m * 2 + 2)
                dve.wait_ge(s_pj, m + 1)
                dve.wait_ge(s_p23, m)
                dve.wait_ge(s_f23, m)
                ve.tensor_tensor(rest_t[:].rearrange("p a b -> p (a b)"), bank[6][0:HALF, 0:2 * N],
                                 parts[:, 0].rearrange("p a b -> p (a b)"), ALU.subtract)
                ve.tensor_tensor(rest_j[:], bank[7][:, HALF:2 * HALF], f4[half][:, :, 1], ALU.subtract).then_inc(s_rest, 1)

            def combine(step, half, done):
                r = bank[4 + half][:, 0:4 * HALF].rearrange("p (h c) -> p h c", c=4)
                dve.wait_ge(s_r[half], done)
                dve.wait_ge(s_hmt, done_t(half, done))
                ve.tensor_tensor(count_p[:], r[:, :, 0], p_j[half][:], ALU.mult)
                step(ve.tensor_reduce(sum_q[:], r[:, :, 1:4], AX_X, ALU.add))
                ve.tensor_tensor(hm[:, half, :], count_p[:], sum_q[:], ALU.add).then_inc(s_comb[half], 1)

            def done_t(half, done):
                return done

            def add_edge_out(slot, done):
                dve.wait_ge(s_y, done)
                x = x_all[:, slot, :]
                ve.tensor_tensor(x, x, bank[7][:, 2 * HALF:2 * HALF + D], ALU.add).then_inc(s_x2, 1)

            rests(0, 0)
            with dve.Fori(0, B) as b:
                step = own_steps(dve, s_dve, base, 2, b)
                for n in range(2 * QB):
                    half, q = n // QB, n % QB
                    if q == 6:
                        dve.wait_ge(s_pj, b * 2 + half)
                        combine(step, 1 - half, b + half)
                    if q == 8:
                        rests(b * 2 + half + 1, 1 - half)
                    if n == 18:
                        add_edge_out(bass.ds(b, 1), b + 1)
                    if not n % 2:
                        dve.wait_ge(s_zd, b * QB + n // 2 + 1)
                        ve.scalar_tensor_tensor(out=g[n % 8][:], in0=bank[n % 4][:].rearrange("p (h j) -> p h j", h=HB),
                                                scalar=0.0, in1=edge_t_all[:, bass.ds(b, 1), :].broadcast_to([N, HB, N]),
                                                op0=ALU.is_gt, op1=ALU.mult).then_inc(s_gd, 1)
            base += 2 * B
            step = own_steps(dve, s_dve, base)
            combine(step, 1, B)
            add_edge_out(slice(B, B + 1), B + 1)
            dve.wait_ge(s_x2, B + 1)
            base += 1

            with dve.Fori(0, NG) as gi:
                step = own_steps(dve, s_dve, base, V_LN + 1, gi)
                step(norm_relu(step, x_all[:, bass.ds(gi * GB + 1, GB), :], h2_all[:, bass.ds(gi * GB, GB), :],
                               L["sqrt_in"], L["sqrt_out"], gi, None))
                assert step.done[0] == V_LN + 1
            base += NG * (V_LN + 1)
            step = own_steps(dve, s_dve, base)
            ve.tensor_reduce(bn_part[:], h2_all[:].rearrange("p b f -> p f b"), AX_X, ALU.add).then_inc(s_bn, 1)
            dve.wait_ge(s_bnp, 3)
            ve.tensor_scalar(bn_mean_c[:], bank[0][0:D, 64:65], 1.0 / (B * N), None, ALU.mult)
            ve.tensor_scalar(bn_mean_bc[:], bank[0][:, 0:D], 1.0 / (B * N), None, ALU.mult).then_inc(s_bn, 1)
            dve.wait_ge(s_bn, 2)
            for c in range(NG):
                hs = h2_all[:, c * GB:(c + 1) * GB, :]
                step(ve.tensor_tensor(xc[:], hs, bn_mean_bc[:].rearrange("p (o f) -> p o f", o=1).broadcast_to([N, GB, D]), ALU.subtract))
                step(ve.tensor_tensor(sq[:], xc[:], xc[:], ALU.mult))
                if c == 0:
                    step(ve.tensor_copy(tmp[:], sq[:]))
                else:
                    step(ve.tensor_tensor(tmp[:], tmp[:], sq[:], ALU.add))
            ve.tensor_reduce(bn_part[:], tmp[:].rearrange("p b f -> p f b"), AX_X, ALU.add).then_inc(s_bn, 1)
            dve.wait_ge(s_bnp, 4)
            ve.tensor_scalar(bn_v[:, 0:1], bank[0][0:D, 64:65], 1.0 / (B * N), BN_EPS, ALU.mult, ALU.add).then_inc(s_bn, 1)
            dve.wait_ge(s_bna, 2)
            dve.wait_ge(s_bn, 4)
            inverse_root(step, bn_v[:, 0:1], bn_v[:, 1:2], bn_v[:, 2:3], bn_v[:, 3:4], bn_v[:, 4:5])
            step(ve.tensor_tensor(bn_v[:, 5:6], bn_v[:, 2:3], bn_v[:, 3:4], ALU.mult))
            step(ve.tensor_tensor(bn_v[:, 6:7], bn_v[:, 5:6], gamma_c[:], ALU.mult))
            step(ve.tensor_scalar(ws3[:], w3[:], bn_v[:, 6:7], None, ALU.mult))
            dve.wait_ge(s_bnp, 5)
            ve.tensor_tensor(cb3[:], bank[1][:, 0:D], b3_bc[:], ALU.add).then_inc(s_bn, 1)
            dve.wait_ge(s_bn, 5)
            base += step.done[0]

            with dve.Fori(0, NG // 2) as t:
                for u in range(2):
                    gi = t * 2 + u
                    step = own_steps(dve, s_dve, base + u * V_P2, 2 * V_P2, t)
                    x = x_all[:, bass.ds(gi * GB + 1, GB), :]
                    dve.wait_ge(L["h3t_psum"], gi)
                    ve.tensor_copy(hn[:], h2_all[:, bass.ds(gi * GB, GB), :]).then_inc(L["dt_used"], 1)
                    dve.wait_ge(s_a2[u], t * 16 + 16)
                    ve.tensor_reduce(stat[:, 2, :], abuf[u][:], AX_X, ALU.add).then_inc(L["sqrt_in"], 1)
                    dve.wait_ge(L["sqrt_in"], NG + gi * 2 + 1)
                    dve.wait_ge(L["sqrt_out"], NG + gi * 2 + 1)
                    inverse_root(step, stat[:, 2, :], stat[:, 3, :], stat[:, 4, :], stat[:, 5, :], stat[:, 6, :])
                    step(ve.tensor_tensor(stat[:, 8, :], stat[:, 4, :], stat[:, 5, :], ALU.mult))
                    step(ve.tensor_tensor(stat[:, 9, :], stat[:, 8, :], stat[:, 2, :], ALU.mult))
                    dve.wait_ge(L["dt_psum"], gi + 1)
                    dve.wait_ge(L["e_psum"], gi)
                    ve.tensor_scalar(d_t[:].rearrange("p b k -> p (b k)"), bank[1][0:D, :], bn_mean_c[:, 0:1], None,
                                     ALU.subtract).then_inc(L["dt_copied"], 1)
                    dve.wait_ge(L["x_psum"], gi + 1)
                    dve.wait_ge(L["elu_exp"], gi)
                    step(ve.tensor_tensor(xl[:], bank[6][:, 0:GB * D].rearrange("p (b f) -> p b f", b=GB),
                                          cb3[:].rearrange("p (o f) -> p o f", o=1).broadcast_to([N, GB, D]), ALU.add))
                    ve.tensor_tensor(yl[:], xl[:], bc(stat[:, 8, :]), ALU.mult).then_inc(L["y_ready"], 1)
                    dve.wait_ge(L["ay_psum"], gi + 1)
                    step(ve.tensor_tensor(tmp[:], bank[7][:, 0:GB * D].rearrange("p (b f) -> p b f", b=GB),
                                          bc(stat[:, 9, :]), ALU.mult))
                    step(ve.tensor_tensor(sq[:], xl[:], tmp[:], ALU.subtract))
                    step(ve.scalar_tensor_tensor(out=tmp[:], in0=sq[:], scalar=LEAK2, in1=sq[:], op0=ALU.mult, op1=ALU.max))
                    step(ve.tensor_tensor(x, x, tmp[:], ALU.add))
                    norm_relu(step, x, hn[:], L["sqrt_in"], L["sqrt_out"], NG + gi * 2 + 1, L["h3_ready"])
                    step(ve.tensor_scalar(pairs2[:], abuf[u][:], 0.0, NEG_INF, ALU.is_le, ALU.mult))
                    dve.wait_ge(L["at_psum"], gi + 1)
                    ve.memset(stat[:, 12, :], 0.0).then_inc(L["a_used"], 1)
                    dve.wait_ge(L["leaky"], gi + 1)
                    step(ve.scalar_tensor_tensor(out=pt[:], in0=pairs[:], scalar=LEAK3, in1=pairs[:], op0=ALU.mult, op1=ALU.max))
                    step(ve.tensor_tensor(pairs2[:], pairs2[:], pt[:], ALU.add))
                    ve.tensor_reduce(stat[:, 9, :], pairs2[:], AX_X, ALU.max, negate=True).then_inc(L["max_ready"], 1)
                    dve.wait_ge(L["exp_done"], gi + 1)
                    step(ve.reciprocal(stat[:, 11, :], stat[:, 10, :]))
                    dve.wait_ge(L["att_psum"], gi + 1)
                    step(ve.tensor_tensor(xl[:], bank[6][:, 0:GB * D].rearrange("p (b f) -> p b f", b=GB),
                                          bc(stat[:, 11, :]), ALU.mult))
                    ve.tensor_scalar(tmp[:], xl[:], 0.0, None, ALU.min).then_inc(L["att_scaled"], 1)
                    step(ve.scalar_tensor_tensor(out=sq[:], in0=xl[:], scalar=0.0, in1=x, op0=ALU.max, op1=ALU.add))
                    dve.wait_ge(L["elu_exp"], gi + 1)
                    dve.wait_ge(s_out[u], t * 16)
                    ve.scalar_tensor_tensor(out=outb[u][:], in0=yl[:], scalar=-1.0, in1=sq[:], op0=ALU.add,
                                            op1=ALU.add).then_inc(L["out_ready"], 1)
                    assert step.done[0] == V_P2, step.done


_INS = ['x', 'adj', 'L1_gnn_W1', 'L1_gnn_b1', 'L1_gnn_W2', 'L1_gnn_b2', 'L2_gnn_gamma', 'L2_gnn_beta',
        'L2_gnn_W', 'L2_gnn_b', 'L3_gnn_W', 'L3_gnn_a']


def kernel(**inputs):
    import numpy as np
    import concourse.bacc as bacc
    from concourse.bass_utils import run_bass_kernel_spmd

    nc = bacc.Bacc("TRN2", target_bir_lowering=False, num_devices=1)
    arrays, args = {}, []
    for name in _INS:
        a = np.ascontiguousarray(inputs[name])
        arrays[f"in_{name}"] = a
        args.append(nc.dram_tensor(f"in_{name}", a.shape, mybir.dt.from_np(a.dtype), kind="ExternalInput").ap())
    out = nc.dram_tensor("out", (B, N, D), F32, kind="ExternalOutput").ap()
    layers(nc, *args, out)
    r = run_bass_kernel_spmd(nc, [arrays], core_ids=[0])
    return r.results[0]["out"]
```

```python
from contextlib import ExitStack

import concourse.bass as bass
from concourse import mybir

F32 = mybir.dt.float32
BF16 = mybir.dt.bfloat16
ALU = mybir.AluOpType
ACT = mybir.ActivationFunctionType
AX_X = mybir.AxisListType.X

B, N, D, H = 64, 128, 64, 192
GB = 4
NG = B // GB
HALF = H // 2
HB = 4
QB = HALF // HB
OH = 32
NOH = HALF // OH
KZ = 3 * OH + 3
LAG = 3
LN_EPS = 1e-5
BN_EPS = 1e-5
BIG = 2.0 ** 100
NEG_INF = -9000000000000000.0
LEAK2, LEAK3 = 0.01, 0.2


def layers(nc, x_d, adj_d, w1_d, b1_d, w2_d, b2_d, gamma_d, beta_d, w3_d, b3_d, w4_d, a_d, out_d):
    with ExitStack() as ctx:
        def sb(name, shape, dt=F32):
            return ctx.enter_context(nc.sbuf_tensor(name, shape, dt))

        def sem(name):
            return ctx.enter_context(nc.semaphore(name))

        bank = [ctx.enter_context(nc.psum_tensor(f"bank{i}", [128, 512], F32)) for i in range(8)]

        ident = sb("ident", [N, N])
        negbig_ident = sb("negbig_ident", [N, N], BF16)
        ones_bf = sb("ones_bf", [N, N], BF16)
        ones_f = sb("ones_f", [N, N])
        w1a = sb("w1a", [D, H])
        w1b = sb("w1b", [D, H])
        w_t = sb("w_t", [D + 1, 2, 2, HALF])
        w_j = sb("w_j", [D + 1, 2, 2, HALF])
        w2 = sb("w2", [HALF, 2, D])
        b2_bc = sb("b2_bc", [N, D])
        gamma_c = sb("gamma_c", [D, 1])
        beta_c = sb("beta_c", [D, 1])
        w3 = sb("w3", [D, D])
        b3_bc = sb("b3_bc", [N, D])
        w4 = sb("w4", [D, D])
        w4_t = sb("w4_t", [D, D])
        a_c = sb("a_c", [D, 2])
        wa_bc = sb("wa_bc", [D, 2, N])
        x_all = sb("x_all", [N, B + 1, D])
        h_t_all = sb("h_t_all", [D + 1, B + 1, N])
        h2_all = sb("h2_all", [N, B, D])
        edge_t_all = sb("edge_t_all", [N, B, N], BF16)
        no_edge_t_all = sb("no_edge_t_all", [N, B, N], BF16)
        def two(name, shape, dt=F32):
            return [sb(f"{name}{u}", shape, dt) for u in range(2)]

        abuf = two("abuf", [N, GB, N])
        a_t = two("a_t", [N, GB, N])
        xc = two("xc", [N, GB, D])
        sq = two("sq", [N, GB, D])
        hn = two("hn", [N, GB, D + 1])
        tmp = two("tmp", [N, GB, D])
        stat = two("stat", [N, 12, GB])
        degree_roots = sb("degree_roots", [N, 2, B])
        rhs = [sb(f"rhs{i}", [N, HALF, N], BF16) for i in range(2)]
        lq = [sb(f"lq{i}", [KZ, NOH, N], BF16) for i in range(2)]
        f4 = [sb(f"f4_{i}", [N, HALF, 4], BF16) for i in range(2)]
        parts = [sb(f"parts{i}", [HALF, 3, 2, N], BF16) for i in range(2)]
        rest_t = sb("rest_t", [HALF, 2, N])
        rest_j = sb("rest_j", [N, HALF])
        h_t = sb("h_t", [D + 1, N])
        p_j = [sb(f"p_j{i}", [N, HALF]) for i in range(2)]
        g = [sb(f"g{i}", [N, HB, N], BF16) for i in range(8)]
        count_p = sb("count_p", [N, HALF])
        sum_q = sb("sum_q", [N, HALF])
        hm = sb("hm", [N, 2, HALF])
        hm_t = sb("hm_t", [HALF, 2, N])
        wait_carrier = sb("wait_carrier", [N, 1])
        bn_part = sb("bn_part", [N, D])
        bn_parts = sb("bn_parts", [N, 4, D])
        ones_col = sb("ones_col", [N, 1], BF16)
        bn_mean_bc = sb("bn_mean_bc", [N, D])
        bn_mean_c = sb("bn_mean_c", [D, 1])
        bn_v = sb("bn_v", [D, 8])
        ws3 = sb("ws3", [D, D])
        beta_bc = sb("beta_bc", [D, N])
        cb3 = sb("cb3", [N, D])
        norm_stat = sb("norm_stat", [N, 8, B])
        scratch = [rhs[i][:].rearrange("p h j -> p (h j)").bitcast(F32) for i in range(2)]

        def late(start, width, rows=N):
            return [scratch[u][0:rows, start:start + GB * width].rearrange("p (b k) -> p b k", b=GB) for u in range(2)]

        no_edge, pairs, logits, probs_t = (late(GB * N * i, N) for i in range(4))
        d_t, h3_t = (late(GB * N * i, N, D) for i in (4, 5))
        xl, yl, wh, outb = (late(GB * N * 6 + GB * D * i, D) for i in range(4))

        s_w = sem("weights_loaded")
        s_x = sem("x_loaded")
        s_a = [sem(f"adj_loaded{u}") for u in range(2)]
        s_const = sem("constants_made")
        s_ident = sem("identity_made")
        s_pool = sem("pool_steps")
        s_wprep = sem("weights_prepared")
        s_dve = sem("vector_steps")
        s_ones = sem("ones_made")
        def both(prefix, names):
            return {n: [sem(f"{prefix}_{n}{u}") for u in range(2)] for n in names}

        A_V = ("steps", "xc1", "v1", "h0_ready", "a_used", "edges_ready", "xc2", "v2", "h1_ready", "degree_ready")
        A_S = ("at_copied", "sq1", "root1", "sq2", "root2", "degree_root", "h1t_copied")
        A_T = ("at_psum", "l0_psum", "h1t_psum")
        A = both("p0", A_V + A_S + A_T)
        s_p0 = sem("phase0_done")
        s_zd = sem("z_for_vector")
        s_za = sem("z_for_scalar")
        s_zfree = sem("z_operands_free")
        s_gd = sem("g_from_vector")
        s_ga = sem("g_from_scalar")
        s_r = [sem(f"sums_ready{i}") for i in range(2)]
        s_comb = [sem(f"sums_combined{i}") for i in range(2)]
        s_ht = sem("h_t_copied")
        s_ptq = sem("pq_t_psum")
        s_pqj = sem("pq_j_psum")
        s_s1t = sem("first_parts_t")
        s_s1j = sem("first_parts_j")
        s_pj = sem("p_j_copied")
        s_rest_t = sem("rests_t_ready")
        s_rest_j = sem("rests_j_ready")
        s_p23 = sem("parts_ready")
        s_pt = sem("second_parts_t")
        s_pjj = sem("second_parts_j")
        s_f23 = sem("f_parts_ready")
        s_fed = [sem(f"z_operands_loaded{i}") for i in range(2)]
        s_hmt = sem("hm_t_psum")
        s_hmc = sem("hm_t_copied")
        s_y = sem("edge_out_psum")
        s_x2 = sem("x2_ready")
        s_edge0 = sem("edge_phase_prepared")
        s_edge = sem("edge_vector_steps")
        s_bn = sem("bn_vector")
        s_bnp = sem("bn_psum")
        s_bna = sem("bn_scalar")
        L_V = ("steps", "dt_copied", "y_ready", "xc", "v", "h3_ready", "a_used", "max_ready", "att_scaled", "out_ready",
               "h2_ready")
        L_S = ("at_copied", "sq", "root", "h3t_copied", "wh_copied", "e_copied", "exp_done", "pt_copied", "elu_exp")
        L_T = ("at_psum", "dt_psum", "x_psum", "ay_psum", "h3t_psum", "wh_psum", "e_psum", "pt_psum", "att_psum")
        L = both("p2", L_V + L_S + L_T)
        s_sum = sem("norm_differences")
        s_sq = sem("norm_squares")
        s_root = sem("norm_roots")
        s_var = sem("norm_variances")
        s_vn = sem("norm_steps")
        s_out = [sem(f"out_stored{u}") for u in range(2)]
        s_out_free = [sem(f"out_tile_free{u}") for u in range(2)]
        s_a2 = [sem(f"adj_loaded_again{u}") for u in range(2)]

        block = ctx.enter_context(nc.Block())

        def own_steps(eng, s, start, per_round=0, rnd=0):
            done = [0]

            def step(ins):
                done[0] += 1
                ins.then_inc(s, 1)
                eng.wait_ge(s, start + per_round * rnd + done[0])
            step.done = done
            return step

        def in_turn(*programs):
            programs = list(programs)
            while programs:
                programs = [p for p in programs if next(p, self_done) is not self_done]

        self_done = object()

        def piecewise(eng, s, per_round, t):
            done = [0]

            def step(ins):
                done[0] += 1
                ins.then_inc(s, 1)
                yield
                eng.wait_ge(s, t * per_round + done[0] + 1)
            step.done = done
            return step

        def start_at_one(eng, table, names):
            for name in names:
                for u in range(2):
                    eng.sem_inc(table[name][u], 1)

        adj_v = adj_d.rearrange("(g b) i k -> g i b k", b=GB)
        out_v = out_d.rearrange("(g b) j f -> g j b f", b=GB)

        V_LN = 8
        V_P0 = 2 * V_LN + 11
        V_P2 = V_LN + 11

        @block.sync
        def _(sp):
            x_v = x_d.rearrange("b j f -> j b f")
            for c in range(4):
                nb = B // 4
                sp.dma_start(x_all[:, 1 + c * nb:1 + (c + 1) * nb, :], x_v[:, c * nb:(c + 1) * nb, :]).then_inc(s_x, 16)
                if c == 0:
                    for u in range(2):
                        sp.dma_start(abuf[u][:], adj_v[u]).then_inc(s_a[u], 16)
            with sp.Fori(0, NG // 2 - 1) as t:
                for u in range(2):
                    sp.wait_ge(A["a_used"][u], t + 2)
                    sp.dma_start(abuf[u][:], adj_v[bass.ds(t * 2 + u + 2, 1)].rearrange("o i b k -> (o i) b k")).then_inc(s_a[u], 16)

            def feed(m, half):
                sp.wait_ge(s_zfree, m + 1)
                sp.wait_ge(s_p23, m + 1)
                for c in range(3):
                    sp.dma_start(rhs[half][3 * OH + c:3 * OH + c + 1, :, :], parts[half][:, c, 0, :]).then_inc(s_fed[half], 16)
                    for n in range(NOH):
                        sp.dma_start(lq[half][OH * c:OH * (c + 1), n, :],
                                     parts[half][OH * n:OH * (n + 1), c, 1, :]).then_inc(s_fed[half], 16)

            sp.wait_ge(s_const, 1)
            feed(0, 0)
            feed(1, 1)
            with sp.Fori(0, B) as b:
                for half in range(2):
                    feed(b * 2 + half + 2, half)

            for u in range(2):
                sp.wait_ge(A["a_used"][u], NG // 2 + 1)
                sp.dma_start(abuf[u][:], adj_v[u]).then_inc(s_a2[u], 16)

            def store(gi, u, t):
                sp.wait_ge(L["out_ready"][u], t + 2)
                sp.dma_start(out_v[bass.ds(gi, 1)].rearrange("o j b f -> (o j) b f"), outb[u]).then_inc(s_out[u], 16)
                sp.wait_ge(s_out[u], t * 16 + 16)
                sp.sem_inc(s_out_free[u], 1)

            for u in range(2):
                sp.sem_inc(s_out_free[u], 1)
            with sp.Fori(0, NG // 2 - 1) as t:
                for u in range(2):
                    sp.wait_ge(L["a_used"][u], t + 2)
                    sp.dma_start(abuf[u][:], adj_v[bass.ds(t * 2 + u + 2, 1)].rearrange("o i b k -> (o i) b k")).then_inc(s_a2[u], 16)
                for u in range(2):
                    store(t * 2 + u, u, t)
            for u in range(2):
                store(NG - 2 + u, u, NG // 2 - 1)
            for u in range(2):
                sp.wait_ge(s_out[u], 16 * (NG // 2))

        @block.gpsimd
        def _(pool):
            step = own_steps(pool, s_pool, 0)
            gp = nc.gpsimd
            step(gp.memset(ident[:], 0.0))
            gp.affine_select(out=ident[:], in_=ident[:], compare_op=ALU.not_equal, fill=1.0, base=0,
                             pattern=[[-1, N]], channel_multiplier=1).then_inc(s_ident, 1)
            pool.wait_ge(s_ident, 1)
            step(gp.memset(negbig_ident[:], 0.0))
            step(gp.affine_select(out=negbig_ident[:], in_=negbig_ident[:], compare_op=ALU.not_equal, fill=-BIG, base=0,
                                  pattern=[[-1, N]], channel_multiplier=1))
            step(gp.memset(ones_bf[:], 1.0))
            for i in range(2):
                step(gp.memset(rhs[i][0:KZ], 0.0))
                for c in range(3):
                    v = rhs[i][OH * c:OH * (c + 1)].rearrange("p (n h) j -> p n h j", h=OH)
                    step(gp.affine_select(out=v, in_=v, compare_op=ALU.not_equal, fill=1.0, base=0,
                                          pattern=[[0, NOH], [-1, OH], [0, N]], channel_multiplier=1))
                step(gp.memset(lq[i][3 * OH:KZ], 1.0))
            gp.memset(ones_f[:], 1.0).then_inc(s_const, 1)

            def later_parts_t(m, half):
                pool.wait_ge(s_rest_t, m + 1)
                gp.tensor_tensor(wait_carrier[:], ones_f[:, 0:1], ones_f[:, 0:1], ALU.mult)
                gp.tensor_copy(parts[half][:, 1], rest_t[:]).then_inc(s_pt, 1)
                pool.wait_ge(s_pt, m + 1)
                gp.tensor_tensor(parts[half][:, 2], rest_t[:], parts[half][:, 1], ALU.subtract).then_inc(s_p23, 1)

            def later_parts_j(m, half):
                pool.wait_ge(s_rest_j, m + 1)
                gp.tensor_tensor(wait_carrier[:], ones_f[:, 0:1], ones_f[:, 0:1], ALU.mult)
                gp.tensor_copy(f4[half][:, :, 2], rest_j[:]).then_inc(s_pjj, 1)
                pool.wait_ge(s_pjj, m + 1)
                gp.tensor_tensor(f4[half][:, :, 3], rest_j[:], f4[half][:, :, 2], ALU.subtract).then_inc(s_f23, 1)

            pool.wait_ge(s_const, 1)
            later_parts_t(0, 0)
            later_parts_t(1, 1)
            later_parts_j(0, 0)
            with pool.Fori(0, B) as b:
                for half in range(2):
                    later_parts_j(b * 2 + half + 1, 1 - half)
                    later_parts_t(b * 2 + half + 2, half)

        @block.scalar
        def _(act):
            sc = nc.scalar

            small = [(w1a[:], w1_d[0:D, :]), (w1b[:], w1_d[D:2 * D, :]),
                     (w_t[D:D + 1, :, 0, :], b1_d.rearrange("(o c h) -> o c h", o=1, c=2)),
                     (w_j[D:D + 1, :, 0, :], b1_d.rearrange("(o c h) -> o c h", o=1, c=2)),
                     (w2[:], w2_d.rearrange("(c h) o -> h c o", c=2)),
                     (b2_bc[:], b2_d.rearrange("(o f) -> o f", o=1).broadcast_to([N, D])),
                     (gamma_c[:], gamma_d.rearrange("(f o) -> f o", o=1)),
                     (beta_c[:], beta_d.rearrange("(f o) -> f o", o=1)),
                     (w3[:], w3_d), (b3_bc[:], b3_d.rearrange("(o f) -> o f", o=1).broadcast_to([N, D])),
                     (w4[:], w4_d), (a_c[:, 0:1], a_d[0:D, :]), (a_c[:, 1:2], a_d[D:2 * D, :])]
            for dst, src in small:
                act.dma_start(dst, src).then_inc(s_w, 16)

            def flat(tile):
                return tile.rearrange("p b k -> p (b k)")

            act.sem_inc(s_ga, 2)
            start_at_one(act, A, A_S)
            start_at_one(act, L, L_S)

            def first_phase(u, t):
                act.wait_ge(A["edges_ready"][u], t + 1)
                act.wait_ge(A["l0_psum"][u], t + 1)
                act.wait_ge(A["at_psum"][u], t + 2)
                sc.copy(flat(a_t[u][:]), bank[4 * u][:]).then_inc(A["at_copied"][u], 1)
                yield
                for k in ("1", "2"):
                    act.wait_ge(A["xc" + k][u], t + 2)
                    sc.square(sq[u][:], xc[u][:]).then_inc(A["sq" + k][u], 1)
                    yield
                    act.wait_ge(A["v" + k][u], t + 2)
                    sc.sqrt(stat[u][:, 3, :], stat[u][:, 2, :]).then_inc(A["root" + k][u], 1)
                    yield
                    if k == "1":
                        act.wait_ge(A["degree_ready"][u], t + 2)
                        sc.sqrt(stat[u][:, 9, :], stat[u][:, 8, :]).then_inc(A["degree_root"][u], 1)
                        yield
                act.wait_ge(A["h1t_psum"][u], t + 2)
                sc.copy(h_t_all[0:D, bass.ds((t * 2 + u) * GB, GB), :],
                        bank[4 * u + 2][0:D, :].rearrange("p (b k) -> p b k", b=GB)).then_inc(A["h1t_copied"][u], 1)
                yield

            with act.Fori(0, NG // 2) as t:
                in_turn(first_phase(0, t), first_phase(1, t))

            def copy_h_t(m, gb):
                act.wait_ge(s_pqj, m)
                sc.copy(h_t[:], h_t_all[:, gb, :]).then_inc(s_ht, 1)

            def first_parts_t(m, half, loaded):
                act.wait_ge(s_ptq, m + 1)
                if loaded is not None:
                    act.wait_ge(s_fed[half], loaded)
                sc.copy(parts[half][:, 0].rearrange("p a b -> p (a b)"), bank[6][0:HALF, 0:2 * N]).then_inc(s_s1t, 1)

            def first_parts_j(m, half, combined):
                act.wait_ge(s_pqj, m + 1)
                if combined is not None:
                    act.wait_ge(s_f23, m)
                sc.copy(f4[half][:, :, 1], bank[7][:, HALF:2 * HALF]).then_inc(s_s1j, 1)
                if combined is not None:
                    act.wait_ge(s_comb[half], combined)
                sc.copy(p_j[half][:], bank[7][:, 0:HALF]).then_inc(s_pj, 1)

            def copy_hm_t(done):
                act.wait_ge(s_hmt, done)
                sc.copy(hm_t[:].rearrange("p c j -> p (c j)"), bank[6][0:HALF, 2 * N:4 * N]).then_inc(s_hmc, 1)

            act.wait_ge(s_p0, 2)
            for u in range(2):
                act.wait_ge(A["h1t_copied"][u], NG // 2 + 1)
            sc.copy(h_t[:], h_t_all[:, 0, :]).then_inc(s_ht, 1)
            for m in range(2):
                first_parts_t(m, m, None)
            first_parts_j(0, 0, None)
            with act.Fori(0, B) as b:
                for n in range(2 * QB):
                    half, q = n // QB, n % QB
                    if q == 2:
                        copy_h_t(b * 2 + half + 1, bass.ds(b + half, 1))
                    if q == 7:
                        first_parts_j(b * 2 + half + 1, 1 - half, b + 1 + half)
                    if q == 9:
                        first_parts_t(b * 2 + half + 2, half, (b + 1) * 16 * 12)
                    if n == 14:
                        copy_hm_t(b + 1)
                    if n % 2:
                        act.wait_ge(s_za, b * QB + n // 2 + 1)
                        sc.activation(g[n % 8][:].rearrange("p h j -> p (h j)"), bank[n % 4][:], ACT.Sign).then_inc(s_ga, 1)
            copy_hm_t(B + 1)

            for c in range(4):
                act.wait_ge(s_sum, c + 1)
                sc.square(scratch[1][:, c * 1024:(c + 1) * 1024], scratch[0][:, c * 1024:(c + 1) * 1024]).then_inc(s_sq, 1)
            act.wait_ge(s_var, 1)
            sc.sqrt(norm_stat[:, 3, :], norm_stat[:, 2, :]).then_inc(s_root, 1)
            act.wait_ge(s_w, 16 * 13)
            sc.copy(beta_bc[:], beta_c[:].broadcast_to([D, N])).then_inc(s_bna, 1)
            for c in range(4):
                act.wait_ge(s_sum, 4 + c + 1)
                sc.square(scratch[1][:, c * 1024:(c + 1) * 1024], scratch[0][:, c * 1024:(c + 1) * 1024]).then_inc(s_sq, 1)
            act.wait_ge(s_bn, 4)
            sc.activation(bn_v[:, 1:2], bn_v[:, 0:1], ACT.Sqrt).then_inc(s_bna, 1)

            def last_phase(u, t):
                act.wait_ge(L["at_psum"][u], t + 2)
                act.wait_ge(L["ay_psum"][u], t + 1)
                sc.copy(flat(a_t[u][:]), bank[4 * u][:]).then_inc(L["at_copied"][u], 1)
                yield
                act.wait_ge(L["xc"][u], t + 2)
                sc.square(sq[u][:], xc[u][:]).then_inc(L["sq"][u], 1)
                yield
                act.wait_ge(L["v"][u], t + 2)
                sc.sqrt(stat[u][:, 3, :], stat[u][:, 2, :]).then_inc(L["root"][u], 1)
                yield
                act.wait_ge(L["h3t_psum"][u], t + 2)
                sc.copy(flat(h3_t[u]), bank[4 * u + 1][0:D, :]).then_inc(L["h3t_copied"][u], 1)
                yield
                act.wait_ge(L["wh_psum"][u], t + 2)
                act.wait_ge(L["att_psum"][u], t + 1)
                sc.copy(flat(wh[u]), bank[4 * u + 2][:, 0:GB * D]).then_inc(L["wh_copied"][u], 1)
                act.wait_ge(L["e_psum"][u], t + 2)
                sc.copy(pairs[u].rearrange("p b k -> p (b k)"), bank[4 * u][:]).then_inc(L["e_copied"][u], 1)
                yield
                act.wait_ge(L["max_ready"][u], t + 2)
                for i in range(GB):
                    last = sc.activation(pairs[u][:, i, :], logits[u][:, i, :], ACT.Exp, bias=stat[u][:, 9, i:i + 1],
                                         accum_out=stat[u][:, 10, i:i + 1])
                last.then_inc(L["exp_done"][u], 1)
                yield
                act.wait_ge(L["pt_psum"][u], t + 2)
                sc.copy(probs_t[u].rearrange("p b k -> p (b k)"), bank[4 * u + 1][:]).then_inc(L["pt_copied"][u], 1)
                yield
                act.wait_ge(L["att_scaled"][u], t + 2)
                sc.activation(yl[u], tmp[u][:], ACT.Exp).then_inc(L["elu_exp"][u], 1)
                yield

            with act.Fori(0, NG // 2) as t:
                in_turn(last_phase(0, t), last_phase(1, t))

        @block.tensor
        def _(pe):
            te = nc.tensor

            start_at_one(pe, A, A_T)
            start_at_one(pe, L, L_T)

            def first_phase(u, t):
                pe.wait_ge(A["at_copied"][u], t + 1)
                pe.wait_ge(s_a[u], t * 16 + 16)
                for i in range(GB):
                    last = te.transpose(bank[4 * u][:, N * i:N * (i + 1)], abuf[u][:, i, :], ident[:])
                last.then_inc(A["at_psum"][u], 1)
                yield
                pe.wait_ge(A["edges_ready"][u], t + 2)
                pe.wait_ge(A["at_copied"][u], t + 2)
                pe.wait_ge(A["h0_ready"][u], t + 2)
                for i in range(GB):
                    te.matmul(bank[4 * u + 1][:, (D + 1) * i:(D + 1) * (i + 1)], a_t[u][:, i, :], hn[u][:, i, :],
                              start=True, stop=True)
                for i in range(GB):
                    last = te.matmul(bank[4 * u + 1][:, (D + 1) * GB + i:(D + 1) * GB + i + 1],
                                     edge_t_all[:, bass.ds((t * 2 + u) * GB + i, 1), :].rearrange("p o k -> p (o k)"),
                                     ones_col[:], start=True, stop=True)
                last.then_inc(A["l0_psum"][u], 1)
                yield
                pe.wait_ge(A["h1t_copied"][u], t + 1)
                pe.wait_ge(A["h1_ready"][u], t + 2)
                te.matmul(bank[4 * u + 2][:, 511:512], ident[:], ident[:, 0:1], start=True, stop=True)
                for i in range(GB):
                    last = te.transpose(bank[4 * u + 2][0:D, N * i:N * (i + 1)], hn[u][:, i, 0:D], ident[:])
                last.then_inc(A["h1t_psum"][u], 1)
                yield

            pe.wait_ge(s_ident, 1)
            pe.wait_ge(s_ones, 1)
            with pe.Fori(0, NG // 2) as t:
                in_turn(first_phase(0, t), first_phase(1, t))

            pe.wait_ge(s_const, 1)
            pe.wait_ge(s_w, 16 * 13)
            pe.wait_ge(s_p0, 1)
            te.transpose(bank[0][0:D, 0:D], w4[:], ident[0:D, 0:D]).then_inc(s_bnp, 1)
            pe.wait_ge(s_wprep, 1)
            te.matmul(bank[0][0:D, 64:66], w4_t[:], a_c[:], start=True, stop=True).then_inc(s_bnp, 1)
            pe.wait_ge(s_wprep, 2)

            def project_t(m, half, gb):
                if m is not None:
                    pe.wait_ge(s_rest_t, m)
                for k in range(2):
                    last = te.matmul(bank[6][0:HALF, N * k:N * (k + 1)], w_t[:, half, k, :], h_t_all[:, gb, :],
                                     start=True, stop=True)
                last.then_inc(s_ptq, 1)

            def project_j(m, half):
                pe.wait_ge(s_ht, m + 1)
                te.matmul(bank[7][:, 0:2 * HALF], h_t[:], w_j[:, half].rearrange("p a b -> p (a b)"),
                          start=True, stop=True).then_inc(s_pqj, 1)

            def edge_out_t(done, rests):
                pe.wait_ge(s_comb[1], done)
                pe.wait_ge(s_rest_t, rests)
                for k in range(2):
                    last = te.transpose(bank[6][0:HALF, 2 * N + N * k:2 * N + N * (k + 1)], hm[:, k, :], ident[:])
                last.then_inc(s_hmt, 1)

            def edge_out(done, rests):
                pe.wait_ge(s_hmc, done)
                pe.wait_ge(s_rest_j, rests)
                for k in range(2):
                    last = te.matmul(bank[7][:, 2 * HALF:2 * HALF + D], hm_t[:, k, :], w2[:, k, :], start=(k == 0), stop=(k == 1))
                last.then_inc(s_y, 1)

            pe.wait_ge(s_edge0, 1)
            for u in range(2):
                pe.wait_ge(A["h1t_copied"][u], NG // 2 + 1)
            pe.sem_inc(s_zfree, 2)
            for m in range(2):
                project_t(m if m else None, m, 0)
            project_j(0, 0)
            with pe.Fori(0, B) as b:
                def masked_sum(n, rnd):
                    half, q = n // QB, n % QB
                    if q == 0:
                        pe.wait_ge(s_comb[half], rnd + 1)
                        pe.wait_ge(s_f23, rnd * 2 + half + 1)
                        te.matmul(bank[4 + half][:, 0:4 * HALF].rearrange("p (a o c) -> p a o c", o=2, c=4 * HB)[:, :, 1, :],
                                  ones_bf[:],
                                  f4[half][:].rearrange("p (a o h) c -> p a o (h c)", o=2, h=HB)[:, :, 1, :],
                                  start=True, stop=True, skip_group_check=True)
                    pe.wait_ge(s_ga if n % 2 else s_gd, rnd * QB + n // 2 + 3)
                    for i in range(HB):
                        h = q * HB + i
                        last = te.matmul(bank[4 + half][:, 4 * h:4 * h + 4], g[n % 8][:, i, :], f4[half][:, h, :],
                                         start=False, stop=True, skip_group_check=True)
                    if q == QB - 1:
                        last.then_inc(s_r[half], 1)

                for n in range(2 * QB):
                    half, q = n // QB, n % QB
                    if q == 4:
                        pe.wait_ge(s_rest_j, b * 2 + half + 1)
                        if half:
                            pe.wait_ge(s_x2, b + 1)
                        project_j(b * 2 + half + 1, 1 - half)
                    if q == 6:
                        if half:
                            pe.wait_ge(s_hmc, b + 1)
                        project_t(b * 2 + half + 2, half, bass.ds(b + 1, 1))
                    if n == 13:
                        edge_out_t(b + 1, b * 2 + 3)
                    if n == 17:
                        edge_out(b + 1, b * 2 + 2)
                    if q == 0:
                        pe.wait_ge(s_fed[half], b * 16 * 12 + 16 * 12)
                    pe.wait_ge(s_ga if n % 2 else s_gd, b * QB + n // 2 + 1)
                    last = te.matmul(bank[n % 4][:], lq[half][:, q * HB // OH, :],
                                     rhs[half][0:KZ, q * HB:(q + 1) * HB, :].rearrange("p h j -> p (h j)"),
                                     start=True, stop=not n % 2)
                    if q == QB - 1:
                        last.then_inc(s_zfree, 1)
                    if n % 2:
                        te.matmul(bank[n % 4][:].rearrange("p (h j) -> p h j", h=HB), negbig_ident[:],
                                  no_edge_t_all[:, bass.ds(b, 1), :].broadcast_to([N, HB, N]),
                                  start=False, stop=True).then_inc(s_za, 1)
                    else:
                        last.then_inc(s_zd, 1)
                    if n >= LAG:
                        masked_sum(n - LAG, b)
                    else:
                        masked_sum(n - LAG + 2 * QB, b - 1)
            for n in range(2 * QB - LAG, 2 * QB):
                masked_sum(n, B - 1)
            edge_out_t(B + 1, 2 * B + 2)
            edge_out(B + 1, 2 * B + 1)

            pe.wait_ge(s_bn, 1)
            te.matmul(bank[0][:, 0:D], ones_f[:], bn_part[:], start=True, stop=True)
            te.matmul(bank[0][0:D, 64:65], bn_part[:], ones_f[:, 0:1], start=True, stop=True).then_inc(s_bnp, 1)
            pe.wait_ge(s_bn, 3)
            te.matmul(bank[0][0:D, 64:65], bn_part[:], ones_f[:, 0:1], start=True, stop=True).then_inc(s_bnp, 1)
            pe.wait_ge(s_bna, 1)
            te.matmul(bank[1][:, 0:D], beta_bc[:], w3[:], start=True, stop=True).then_inc(s_bnp, 1)
            pe.wait_ge(s_bn, 5)

            def last_phase(u, t):
                pe.wait_ge(L["e_copied"][u], t + 1)
                pe.wait_ge(s_a2[u], t * 16 + 16)
                for i in range(GB):
                    last = te.transpose(bank[4 * u][:, N * i:N * (i + 1)], abuf[u][:, i, :], ident[:])
                last.then_inc(L["at_psum"][u], 1)
                yield
                pe.wait_ge(L["pt_copied"][u], t + 1)
                pe.wait_ge(L["h2_ready"][u], t + 2)
                te.matmul(bank[4 * u + 1][:, 511:512], ident[:], ones_f[:, 0:1], start=True, stop=True)
                for i in range(GB):
                    last = te.transpose(bank[4 * u + 1][0:D, N * i:N * (i + 1)], hn[u][:, i, 0:D], ident[:])
                last.then_inc(L["dt_psum"][u], 1)
                yield
                pe.wait_ge(L["att_scaled"][u], t + 1)
                pe.wait_ge(L["dt_copied"][u], t + 2)
                for i in range(GB):
                    last = te.matmul(bank[4 * u + 2][:, D * i:D * (i + 1)], d_t[u][:, i, :], ws3[:], start=True, stop=True)
                last.then_inc(L["x_psum"][u], 1)
                yield
                pe.wait_ge(L["at_copied"][u], t + 2)
                pe.wait_ge(L["y_ready"][u], t + 2)
                for i in range(GB):
                    last = te.matmul(bank[4 * u + 3][:, D * i:D * (i + 1)], a_t[u][:, i, :], yl[u][:, i, :], start=True, stop=True)
                last.then_inc(L["ay_psum"][u], 1)
                yield
                pe.wait_ge(L["h3_ready"][u], t + 2)
                te.matmul(bank[4 * u + 1][:, 511:512], ident[:], ones_f[:, 0:1], start=True, stop=True)
                for i in range(GB):
                    last = te.transpose(bank[4 * u + 1][0:D, N * i:N * (i + 1)], hn[u][:, i, 0:D], ident[:])
                last.then_inc(L["h3t_psum"][u], 1)
                yield
                pe.wait_ge(L["h3t_copied"][u], t + 2)
                for i in range(GB):
                    last = te.matmul(bank[4 * u + 2][:, D * i:D * (i + 1)], h3_t[u][:, i, :], w4[:], start=True, stop=True)
                last.then_inc(L["wh_psum"][u], 1)
                for i in range(GB):
                    te.matmul(bank[4 * u][:, N * i:N * (i + 1)], h3_t[u][:, i, :], wa_bc[:, 0, :], start=True, stop=False)
                    last = te.matmul(bank[4 * u][:, N * i:N * (i + 1)], wa_bc[:, 1, :], h3_t[u][:, i, :], start=False, stop=True)
                last.then_inc(L["e_psum"][u], 1)
                yield
                pe.wait_ge(L["exp_done"][u], t + 2)
                for i in range(GB):
                    last = te.transpose(bank[4 * u + 1][:, N * i:N * (i + 1)], pairs[u][:, i, :], ident[:])
                last.then_inc(L["pt_psum"][u], 1)
                yield
                pe.wait_ge(L["wh_copied"][u], t + 2)
                pe.wait_ge(L["pt_copied"][u], t + 2)
                for i in range(GB):
                    last = te.matmul(bank[4 * u + 2][:, D * i:D * (i + 1)], probs_t[u][:, i, :], wh[u][:, i, :], start=True, stop=True)
                last.then_inc(L["att_psum"][u], 1)
                yield

            with pe.Fori(0, NG // 2) as t:
                in_turn(last_phase(0, t), last_phase(1, t))

        @block.vector
        def _(dve):
            ve = nc.vector

            def bc(col, n=D, m=GB):
                return col.rearrange("p (b o) -> p b o", o=1).broadcast_to([N, m, n])

            def inverse_root(step, v, root, r, t, u, out):
                yield from step(ve.reciprocal(r, root))
                yield from step(ve.tensor_tensor(t, r, r, ALU.mult))
                yield from step(ve.tensor_tensor(u, t, v, ALU.mult))
                yield from step(ve.tensor_scalar(t, u, -0.5, 1.5, ALU.mult, ALU.add))
                yield from step(ve.tensor_tensor(out, r, t, ALU.mult))

            def norm_relu(step, x, u, t, s_xc, s_sq, s_v, s_root, s_done):
                st = stat[u]
                ve.memset(st[:, 11, :], 0.0)
                yield from step(ve.tensor_reduce(st[:, 0, :], x, AX_X, ALU.add))
                yield from step(ve.tensor_scalar(st[:, 1, :], st[:, 0, :], 1.0 / D, None, ALU.mult))
                ve.tensor_tensor(xc[u][:], x, bc(st[:, 1, :]), ALU.subtract).then_inc(s_xc, 1)
                yield
                dve.wait_ge(s_sq, t + 2)
                yield from step(ve.tensor_reduce(st[:, 0, :], sq[u][:], AX_X, ALU.add))
                ve.tensor_scalar(st[:, 2, :], st[:, 0, :], 1.0 / D, LN_EPS, ALU.mult, ALU.add).then_inc(s_v, 1)
                yield
                dve.wait_ge(s_v, t + 2)
                dve.wait_ge(s_root, t + 2)
                yield from inverse_root(step, st[:, 2, :], st[:, 3, :], st[:, 4, :], st[:, 5, :], st[:, 6, :], st[:, 7, :])
                ve.scalar_tensor_tensor(out=hn[u][:, :, 0:D], in0=xc[u][:], scalar=0.0, in1=bc(st[:, 7, :]),
                                        op0=ALU.max, op1=ALU.mult).then_inc(s_done, 1)

            def whole(program):
                for _ in program:
                    pass

            def waiting(step):
                def run(ins):
                    step(ins)
                    return iter(())
                return run

            start_at_one(dve, A, A_V)
            start_at_one(dve, L, L_V)
            dve.sem_inc(s_comb[0], 1)
            dve.sem_inc(s_gd, 2)
            for u in range(2):
                ve.memset(hn[u][:, :, D:D + 1], 1.0)
            ve.memset(ones_col[:], 1.0).then_inc(s_ones, 1)
            step = own_steps(dve, s_dve, 0)
            dve.wait_ge(s_w, 16 * 13)
            wa = w1a[:].rearrange("p (c h) -> p c h", c=2)
            wb = w1b[:].rearrange("p (c h) -> p c h", c=2)
            ve.tensor_tensor(w_t[0:D, :, 0, :], wa, wb, ALU.add).then_inc(s_edge0, 1)
            ve.tensor_tensor(w_j[0:D, :, 0, :], wa, wb, ALU.add)
            ve.tensor_scalar(w_t[0:D, :, 1, :], wb, -1.0, None, ALU.mult)
            wbq = wb.rearrange("p c (a o h) -> p (c a) o h", o=2, h=HB)
            wjq = w_j[0:D, :, 1, :].rearrange("p c (a o h) -> p c a o h", o=2, h=HB)
            for c in range(2):
                for o in range(2):
                    ve.tensor_scalar(wjq[:, c, :, o, :], wbq[:, c * (QB // 2):(c + 1) * (QB // 2), o, :],
                                     -1.0 if o == 0 else -0.5, None, ALU.mult)
                fq = f4[c][:].rearrange("p (a o h) c -> p a o h c", o=2, h=HB)
                ve.memset(fq[:, :, 0, :, 0], 1.0)
                ve.memset(fq[:, :, 1, :, 0], 0.5)
                ve.memset(p_j[c][:], 0.0)
            ve.memset(w_t[D:D + 1, :, 1, :], 0.0)
            ve.memset(w_j[D:D + 1, :, 1, :], 0.0)
            ve.memset(h_t_all[D:D + 1, :, :], 1.0)
            ve.memset(h_t_all[0:D, B, :], 0.0)
            ve.memset(hm[:], 0.0)
            for i in range(8):
                ve.memset(g[i][:], 0.0)
            ve.memset(f4[1][:, :, 1:4], 0.0)
            ve.memset(x_all[:, 0, :], 0.0).then_inc(s_p0, 1)

            def first_phase(u, t):
                step = piecewise(dve, A["steps"][u], V_P0, t)
                st = stat[u]
                x = x_all[:, bass.ds((t * 2 + u) * GB + 1, GB), :]
                dve.wait_ge(A["h1t_psum"][u], t + 1)
                yield from norm_relu(step, x, u, t, A["xc1"][u], A["sq1"][u], A["v1"][u], A["root1"][u], A["h0_ready"][u])
                yield
                dve.wait_ge(A["at_copied"][u], t + 2)
                ve.tensor_scalar(edge_t_all[:, bass.ds((t * 2 + u) * GB, GB), :], a_t[u][:], 0.0, None, ALU.is_gt)
                ve.tensor_scalar(no_edge_t_all[:, bass.ds((t * 2 + u) * GB, GB), :], a_t[u][:], 0.0, None, ALU.is_le)\
                    .then_inc(A["edges_ready"][u], 1)
                yield
                dve.wait_ge(A["at_psum"][u], t + 2)
                ve.memset(st[:, 11, :], 0.0).then_inc(A["a_used"][u], 1)
                dve.wait_ge(A["l0_psum"][u], t + 2)
                sums = bank[4 * u + 1][:, 0:GB * (D + 1)].rearrange("p (b f) -> p b f", b=GB)
                ve.tensor_copy(st[:, 8, :], sums[:, :, D]).then_inc(A["degree_ready"][u], 1)
                yield
                yield from step(ve.tensor_scalar(st[:, 10, :], sums[:, :, D], 1.0, None, ALU.max))
                yield from step(ve.reciprocal(st[:, 6, :], st[:, 10, :]))
                yield from step(ve.tensor_tensor(tmp[u][:], sums[:, :, 0:D], bc(st[:, 6, :]), ALU.mult))
                yield from step(ve.tensor_tensor(x, x, tmp[u][:], ALU.add))
                yield from step(ve.tensor_copy(st[:, 10, :], bank[4 * u + 1][:, GB * (D + 1):GB * (D + 2)]))
                yield from norm_relu(step, x, u, t, A["xc2"][u], A["sq2"][u], A["v2"][u], A["root2"][u], A["h1_ready"][u])
                ve.tensor_tensor(tmp[u][:], b2_bc[:].rearrange("p (o f) -> p o f", o=1).broadcast_to([N, GB, D]),
                                 bc(st[:, 10, :]), ALU.mult)
                dve.wait_ge(A["degree_root"][u], t + 2)
                yield from inverse_root(step, st[:, 8, :], st[:, 9, :], st[:, 4, :], st[:, 5, :], st[:, 6, :],
                                        degree_roots[:, 0, bass.ds((t * 2 + u) * GB, GB)])
                ve.tensor_tensor(degree_roots[:, 1, bass.ds((t * 2 + u) * GB, GB)],
                                 degree_roots[:, 0, bass.ds((t * 2 + u) * GB, GB)], st[:, 8, :], ALU.mult)
                ve.tensor_tensor(x, x, tmp[u][:], ALU.add).then_inc(A["steps"][u], 1)
                step.done[0] += 1
                dve.wait_ge(A["steps"][u], t * V_P0 + step.done[0] + 1)
                assert step.done[0] == V_P0, step.done

            dve.wait_ge(s_x, 64)
            with dve.Fori(0, NG // 2) as t:
                in_turn(first_phase(0, t), first_phase(1, t))
            for i in (4, 5):
                step(ve.memset(bank[i][:], 0.0))
            ve.memset(stat[0][:, 11, :], 0.0).then_inc(s_p0, 1)
            dve.wait_ge(s_bnp, 1)
            ve.tensor_copy(w4_t[:], bank[0][0:D, 0:D]).then_inc(s_wprep, 1)
            dve.wait_ge(s_bnp, 2)
            step(ve.tensor_copy(bn_v[:, 0:2], bank[0][0:D, 64:66]))
            for k in range(2):
                last = ve.tensor_copy(wa_bc[:, k, :], bn_v[:, k:k + 1].broadcast_to([D, N]))
            last.then_inc(s_wprep, 1)

            def rests_t(m, half):
                dve.wait_ge(s_s1t, m + 1)
                if not isinstance(m, int) or m:
                    dve.wait_ge(s_p23, m)
                ve.tensor_tensor(rest_t[:].rearrange("p a b -> p (a b)"), bank[6][0:HALF, 0:2 * N],
                                 parts[half][:, 0].rearrange("p a b -> p (a b)"), ALU.subtract).then_inc(s_rest_t, 1)

            def rests_j(m, half):
                dve.wait_ge(s_s1j, m + 1)
                dve.wait_ge(s_pj, m + 1)
                if not isinstance(m, int) or m:
                    dve.wait_ge(s_f23, m)
                ve.tensor_tensor(rest_j[:], bank[7][:, HALF:2 * HALF], f4[half][:, :, 1], ALU.subtract).then_inc(s_rest_j, 1)

            def combine(step, half, done):
                r = bank[4 + half][:, 0:4 * HALF].rearrange("p (h c) -> p h c", c=4)
                dve.wait_ge(s_r[half], done)
                if half == 0:
                    dve.wait_ge(s_hmt, done)
                ve.tensor_tensor(count_p[:], r[:, :, 0], p_j[half][:], ALU.mult)
                step(ve.tensor_reduce(sum_q[:], r[:, :, 1:4], AX_X, ALU.add))
                ve.tensor_tensor(hm[:, half, :], count_p[:], sum_q[:], ALU.add).then_inc(s_comb[half], 1)

            def add_edge_out(slot, done):
                dve.wait_ge(s_y, done)
                x = x_all[:, slot, :]
                ve.tensor_tensor(x, x, bank[7][:, 2 * HALF:2 * HALF + D], ALU.add).then_inc(s_x2, 1)

            for m in range(2):
                rests_t(m, m)
            rests_j(0, 0)
            with dve.Fori(0, B) as b:
                step = own_steps(dve, s_edge, 0, 2, b)
                for n in range(2 * QB):
                    half, q = n // QB, n % QB
                    if q == 6:
                        combine(step, 1 - half, b + 1)
                    if q == 9:
                        rests_j(b * 2 + half + 1, 1 - half)
                    if q == 11:
                        rests_t(b * 2 + half + 2, half)
                    if n == 21:
                        add_edge_out(bass.ds(b, 1), b + 1)
                    if not n % 2:
                        dve.wait_ge(s_zd, b * QB + n // 2 + 1)
                        ve.scalar_tensor_tensor(out=g[n % 8][:], in0=bank[n % 4][:].rearrange("p (h j) -> p h j", h=HB),
                                                scalar=0.0, in1=edge_t_all[:, bass.ds(b, 1), :].broadcast_to([N, HB, N]),
                                                op0=ALU.is_gt, op1=ALU.mult).then_inc(s_gd, 1)
            step = own_steps(dve, s_edge, 2 * B)
            combine(step, 1, B + 1)
            add_edge_out(slice(B, B + 1), B + 1)
            dve.wait_ge(s_x2, B + 1)

            for i in range(2):
                dve.wait_ge(s_fed[i], 16 * 12 * (B + 1))
            step = own_steps(dve, s_vn, 0)
            run = waiting(step)
            ns = norm_stat
            quarters = [slice(c * B // 4, (c + 1) * B // 4) for c in range(4)]

            def chunk(i, c):
                return scratch[i][:, c * 1024:(c + 1) * 1024].rearrange("p (b f) -> p b f", f=D)

            for c, qs in enumerate(quarters):
                last = ve.tensor_reduce(ns[:, 0, qs], x_all[:, 1 + qs.start:1 + qs.stop, :], AX_X, ALU.add)
            step(last)
            step(ve.tensor_scalar(ns[:, 1, :], ns[:, 0, :], 1.0 / D, None, ALU.mult))
            for c, qs in enumerate(quarters):
                ve.tensor_tensor(chunk(0, c), x_all[:, 1 + qs.start:1 + qs.stop, :], bc(ns[:, 1, qs], D, B // 4),
                                 ALU.subtract).then_inc(s_sum, 1)
            for c, qs in enumerate(quarters):
                dve.wait_ge(s_sq, c + 1)
                last = ve.tensor_reduce(ns[:, 0, qs], chunk(1, c), AX_X, ALU.add)
            step(last)
            ve.tensor_scalar(ns[:, 2, :], ns[:, 0, :], 1.0 / D, LN_EPS, ALU.mult, ALU.add).then_inc(s_var, 1)
            dve.wait_ge(s_var, 1)
            dve.wait_ge(s_root, 1)
            whole(inverse_root(run, ns[:, 2, :], ns[:, 3, :], ns[:, 4, :], ns[:, 5, :], ns[:, 6, :], ns[:, 7, :]))
            for c, qs in enumerate(quarters):
                last = ve.scalar_tensor_tensor(out=h2_all[:, qs, :], in0=chunk(0, c), scalar=0.0,
                                               in1=bc(ns[:, 7, qs], D, B // 4), op0=ALU.max, op1=ALU.mult)
            step(last)
            ve.tensor_reduce(bn_part[:], h2_all[:].rearrange("p b f -> p f b"), AX_X, ALU.add).then_inc(s_bn, 1)
            dve.wait_ge(s_bnp, 3)
            ve.tensor_scalar(bn_mean_c[:], bank[0][0:D, 64:65], 1.0 / (B * N), None, ALU.mult)
            ve.tensor_scalar(bn_mean_bc[:], bank[0][:, 0:D], 1.0 / (B * N), None, ALU.mult).then_inc(s_bn, 1)
            dve.wait_ge(s_bn, 2)
            for c, qs in enumerate(quarters):
                ve.tensor_tensor(chunk(0, c), h2_all[:, qs, :],
                                 bn_mean_bc[:].rearrange("p (o f) -> p o f", o=1).broadcast_to([N, B // 4, D]),
                                 ALU.subtract).then_inc(s_sum, 1)
            for c in range(4):
                dve.wait_ge(s_sq, 4 + c + 1)
                last = ve.tensor_reduce(bn_parts[:, c, :], chunk(1, c).rearrange("p b f -> p f b"), AX_X, ALU.add)
            step(last)
            ve.tensor_reduce(bn_part[:], bn_parts[:].rearrange("p c f -> p f c"), AX_X, ALU.add).then_inc(s_bn, 1)
            dve.wait_ge(s_bnp, 4)
            ve.tensor_scalar(bn_v[:, 0:1], bank[0][0:D, 64:65], 1.0 / (B * N), BN_EPS, ALU.mult, ALU.add).then_inc(s_bn, 1)
            dve.wait_ge(s_bna, 2)
            dve.wait_ge(s_bn, 4)
            whole(inverse_root(run, bn_v[:, 0:1], bn_v[:, 1:2], bn_v[:, 2:3], bn_v[:, 3:4], bn_v[:, 4:5], bn_v[:, 5:6]))
            step(ve.tensor_tensor(bn_v[:, 6:7], bn_v[:, 5:6], gamma_c[:], ALU.mult))
            step(ve.tensor_scalar(ws3[:], w3[:], bn_v[:, 6:7], None, ALU.mult))
            dve.wait_ge(s_bnp, 5)
            ve.tensor_tensor(cb3[:], bank[1][:, 0:D], b3_bc[:], ALU.add).then_inc(s_bn, 1)
            dve.wait_ge(s_bn, 5)

            def last_phase(u, t):
                step = piecewise(dve, L["steps"][u], V_P2, t)
                st = stat[u]
                x = x_all[:, bass.ds((t * 2 + u) * GB + 1, GB), :]
                dve.wait_ge(L["h3t_psum"][u], t + 1)
                ve.tensor_copy(hn[u][:, :, 0:D], h2_all[:, bass.ds((t * 2 + u) * GB, GB), :])
                ve.memset(st[:, 11, :], 0.0).then_inc(L["h2_ready"][u], 1)
                dve.wait_ge(s_a2[u], t * 16 + 16)
                yield from step(ve.tensor_scalar(no_edge[u], abuf[u][:], 0.0, NEG_INF, ALU.is_le, ALU.mult))
                dve.wait_ge(L["at_psum"][u], t + 2)
                ve.memset(st[:, 11, :], 0.0).then_inc(L["a_used"][u], 1)
                dve.wait_ge(L["x_psum"][u], t + 1)
                dve.wait_ge(L["dt_psum"][u], t + 2)
                ve.tensor_scalar(d_t[u].rearrange("p b k -> p (b k)"), bank[4 * u + 1][0:D, :], bn_mean_c[:, 0:1], None,
                                 ALU.subtract).then_inc(L["dt_copied"][u], 1)
                yield
                dve.wait_ge(L["x_psum"][u], t + 2)
                yield from step(ve.tensor_tensor(xl[u], bank[4 * u + 2][:, 0:GB * D].rearrange("p (b f) -> p b f", b=GB),
                                                 cb3[:].rearrange("p (o f) -> p o f", o=1).broadcast_to([N, GB, D]), ALU.add))
                ve.tensor_tensor(yl[u], xl[u], bc(degree_roots[:, 0, bass.ds((t * 2 + u) * GB, GB)]), ALU.mult)\
                    .then_inc(L["y_ready"][u], 1)
                yield
                dve.wait_ge(L["ay_psum"][u], t + 2)
                yield from step(ve.tensor_tensor(tmp[u][:], bank[4 * u + 3][:, 0:GB * D].rearrange("p (b f) -> p b f", b=GB),
                                                 bc(degree_roots[:, 1, bass.ds((t * 2 + u) * GB, GB)]), ALU.mult))
                yield from step(ve.tensor_tensor(xc[u][:], xl[u], tmp[u][:], ALU.subtract))
                yield from step(ve.scalar_tensor_tensor(out=tmp[u][:], in0=xc[u][:], scalar=LEAK2, in1=xc[u][:],
                                                        op0=ALU.mult, op1=ALU.max))
                yield from step(ve.tensor_tensor(x, x, tmp[u][:], ALU.add))
                yield from norm_relu(step, x, u, t, L["xc"][u], L["sq"][u], L["v"][u], L["root"][u], L["h3_ready"][u])
                yield
                dve.wait_ge(L["e_copied"][u], t + 2)
                yield from step(ve.scalar_tensor_tensor(out=logits[u], in0=pairs[u], scalar=LEAK3, in1=pairs[u],
                                                        op0=ALU.mult, op1=ALU.max))
                yield from step(ve.tensor_tensor(logits[u], logits[u], no_edge[u], ALU.add))
                ve.tensor_reduce(st[:, 9, :], logits[u], AX_X, ALU.max, negate=True).then_inc(L["max_ready"][u], 1)
                yield
                dve.wait_ge(L["exp_done"][u], t + 2)
                yield from step(ve.reciprocal(st[:, 8, :], st[:, 10, :]))
                dve.wait_ge(L["att_psum"][u], t + 2)
                yield from step(ve.tensor_tensor(xl[u], bank[4 * u + 2][:, 0:GB * D].rearrange("p (b f) -> p b f", b=GB),
                                                 bc(st[:, 8, :]), ALU.mult))
                ve.tensor_scalar(tmp[u][:], xl[u], 0.0, None, ALU.min).then_inc(L["att_scaled"][u], 1)
                yield from step(ve.scalar_tensor_tensor(out=xc[u][:], in0=xl[u], scalar=0.0, in1=x, op0=ALU.max, op1=ALU.add))
                dve.wait_ge(L["elu_exp"][u], t + 2)
                dve.wait_ge(s_out_free[u], t + 1)
                ve.scalar_tensor_tensor(out=outb[u], in0=yl[u], scalar=-1.0, in1=xc[u][:], op0=ALU.add,
                                        op1=ALU.add).then_inc(L["out_ready"][u], 1)
                assert step.done[0] == V_P2, step.done

            with dve.Fori(0, NG // 2) as t:
                in_turn(last_phase(0, t), last_phase(1, t))


_INS = ['x', 'adj', 'L1_gnn_W1', 'L1_gnn_b1', 'L1_gnn_W2', 'L1_gnn_b2', 'L2_gnn_gamma', 'L2_gnn_beta',
        'L2_gnn_W', 'L2_gnn_b', 'L3_gnn_W', 'L3_gnn_a']


def kernel(**inputs):
    import numpy as np
    import concourse.bacc as bacc
    from concourse.bass_utils import run_bass_kernel_spmd

    nc = bacc.Bacc("TRN2", target_bir_lowering=False, num_devices=1)
    arrays, args = {}, []
    for name in _INS:
        a = np.ascontiguousarray(inputs[name])
        arrays[f"in_{name}"] = a
        args.append(nc.dram_tensor(f"in_{name}", a.shape, mybir.dt.from_np(a.dtype), kind="ExternalInput").ap())
    out = nc.dram_tensor("out", (B, N, D), F32, kind="ExternalOutput").ap()
    layers(nc, *args, out)
    r = run_bass_kernel_spmd(nc, [arrays], core_ids=[0])
    return r.results[0]["out"]
```

```python
from contextlib import ExitStack

import concourse.bass as bass
from concourse import mybir

F32 = mybir.dt.float32
BF16 = mybir.dt.bfloat16
ALU = mybir.AluOpType
ACT = mybir.ActivationFunctionType
AX_X = mybir.AxisListType.X

B, N, D, H = 64, 128, 64, 192
GB = 4
NG = B // GB
U = 4
ROUNDS = NG // U
HALF = H // 2
HB = 4
QB = HALF // HB
OH = 32
NOH = HALF // OH
LAG = 3
LN_EPS = 1e-5
BN_EPS = 1e-5
BIG = 2.0 ** 100
NEG_INF = -9000000000000000.0
LEAK2, LEAK3 = 0.01, 0.2


def layers(nc, x_d, adj_d, w1_d, b1_d, w2_d, b2_d, gamma_d, beta_d, w3_d, b3_d, w4_d, a_d, out_d):
    with ExitStack() as ctx:
        def sb(name, shape, dt=F32):
            return ctx.enter_context(nc.sbuf_tensor(name, shape, dt))

        def sem(name):
            return ctx.enter_context(nc.semaphore(name))

        bank = [ctx.enter_context(nc.psum_tensor(f"bank{i}", [128, 512], F32)) for i in range(8)]

        ident = sb("ident", [N, N])
        negbig_ident = sb("negbig_ident", [N, N], BF16)
        ones_bf = sb("ones_bf", [N, N], BF16)
        ones_f = sb("ones_f", [N, N])
        w1a = sb("w1a", [D, H])
        w1b = sb("w1b", [D, H])
        w_t = sb("w_t", [D + 1, 2, 2, HALF])
        w_j = sb("w_j", [D + 1, 2, 2, HALF])
        w2 = sb("w2", [HALF, 2, D])
        b2_bc = sb("b2_bc", [N, D])
        gamma_c = sb("gamma_c", [2 * D, 1])
        beta_c = sb("beta_c", [2 * D, 1])
        w3 = sb("w3", [2 * D, D])
        b3_bc = sb("b3_bc", [N, D])
        w4 = sb("w4", [2 * D, D])
        w4_pair = sb("w4_pair", [2 * D, 2, D + 2])
        w4_t = sb("w4_t", [D, 2, D])
        a_c = sb("a_c", [D, 2])
        x_all = sb("x_all", [N, B + 1, D])
        h_t_tile = sb("h_t_tile", [N, B + 1, N])
        h_t_all = h_t_tile[0:D + 1]
        h2_all = h_t_tile[:].rearrange("p b n -> p (b n)")[:, 0:B * D].rearrange("p (b f) -> p b f", f=D)
        edge_t_all = sb("edge_t_all", [N, B, N], BF16)
        no_edge_t_all = sb("no_edge_t_all", [N, B, N], BF16)
        def each(name, shape, dt=F32):
            return [sb(f"{name}{u}", shape, dt) for u in range(U)]

        abuf = each("abuf", [N, GB, N])
        a_t = each("a_t", [N, GB, N])
        xc = each("xc", [N, GB, D])
        sq = each("sq", [N, GB, D])
        hn = each("hn", [N, GB, D + 1])
        tmp = each("tmp", [N, GB, D])
        stat = each("stat", [N, 12, GB])
        terms = each("terms", [N, GB, 2])
        degrees = sb("degrees", [N, B])
        degree_roots = sb("degree_roots", [N, 2, B])
        rhs = [sb(f"rhs{i}", [N, HALF, N], BF16) for i in range(2)]
        lq = [sb(f"lq{i}", [N, NOH, N], BF16) for i in range(2)]
        f4 = [sb(f"f4_{i}", [N, HALF, 4], BF16) for i in range(2)]
        parts = [sb(f"parts{i}", [HALF, 3, 2, N], BF16) for i in range(2)]
        rest_t = sb("rest_t", [HALF, 2, N])
        rest_j = sb("rest_j", [N, HALF])
        h_t = sb("h_t", [D + 1, N])
        p_j = [sb(f"p_j{i}", [N, HALF]) for i in range(2)]
        g = [sb(f"g{i}", [N, HB, N], BF16) for i in range(8)]
        count_p = sb("count_p", [N, HALF])
        sum_q = sb("sum_q", [N, HALF])
        hm = sb("hm", [N, 2, HALF])
        hm_t = sb("hm_t", [HALF, 2, N])
        wait_carrier = sb("wait_carrier", [N, 1])
        act_wait_carrier = sb("act_wait_carrier", [N, 1])
        bn_part = sb("bn_part", [N, 2, D])
        bn_parts = sb("bn_parts", [N, 4, D])
        ones_col = sb("ones_col", [N, 1], BF16)
        bn_mean_bc = sb("bn_mean_bc", [N, D])
        bn_mean_c = sb("bn_mean_c", [2 * D, 1])
        bn_v = sb("bn_v", [2 * D, 8])
        ws3_pair = sb("ws3_pair", [2 * D, 2, D])
        shift_bc = sb("shift_bc", [D, N])
        cb3 = sb("cb3", [N, D])
        norm_stat = sb("norm_stat", [N, 8, B])
        scratch = [rhs[i][:].rearrange("p h j -> p (h j)").bitcast(F32) for i in range(2)]

        def late(start, width, graphs=GB):
            tiles = []
            for u in range(U):
                first = (u // 2) * (GB * (4 * N + 4 * D)) + start
                tiles.append(scratch[u % 2][:, first:first + graphs * width].rearrange("p (b k) -> p b k", b=graphs))
            return tiles

        no_edge, pairs, logits, h2_t = late(0, N), late(GB * N, N), late(GB * N * 2, N), late(GB * N * 3, N, GB // 2)
        h2_h3 = late(GB * N * 3 + GB // 2 * N, D)
        probs_t, h3_t = logits, h2_t
        xl, yl, wh, outb = (late(GB * (N * 4 + D * i), D) for i in range(4))

        s_w1 = sem("edge_weights_loaded")
        s_w = sem("weights_loaded")
        s_x = sem("x_loaded")
        s_a = [sem(f"adj_loaded{u}") for u in range(U)]
        s_const = sem("constants_made")
        s_ident = sem("identity_made")
        s_pool = sem("pool_steps")
        s_wprep = sem("weights_prepared")
        s_dve = sem("vector_steps")
        s_ones = sem("ones_made")
        class Points:
            def __init__(self, prefix, **orders):
                self.at, self.order = {}, {}
                for engine, names in orders.items():
                    sems = [sem(f"{prefix}_{engine}{u}") for u in range(U)]
                    for name in names:
                        self.at[name], self.order[name] = sems, names

            def sem(self, name, u):
                return self.at[name][u]

            def before(self, name, t):
                return t * len(self.order[name]) + self.order[name].index(name) + 1

            def now(self, name, t):
                return (t + 1) * len(self.order[name]) + self.order[name].index(name) + 1

            def start(self, eng, name):
                for s in self.at[name]:
                    eng.sem_inc(s, len(self.order[name]))

        A = Points("p0", vector=("xc1", "v1", "h0_ready", "edges_ready", "a_used", "xc2", "v2", "h1_ready"),
                   scalar=("at_copied", "sq1", "root1", "sq2", "root2", "h1t_copied"),
                   tensor=("at_psum", "l0_psum", "h1t_psum"))
        A_steps = [sem(f"p0_vector_steps{u}") for u in range(U)]
        s_p0 = sem("phase0_done")
        s_zd = sem("z_for_vector")
        s_za = sem("z_for_scalar")
        s_zfree_lq = sem("z_first_operands_free")
        s_zfree = sem("z_operands_free")
        s_gd = sem("g_from_vector")
        s_ga = sem("g_from_scalar")
        s_r = [sem(f"sums_ready{i}") for i in range(2)]
        s_comb = [sem(f"sums_combined{i}") for i in range(2)]
        s_ht = sem("h_t_copied")
        s_ptq = sem("pq_t_psum")
        s_pqj = sem("pq_j_psum")
        s_s1t = sem("first_parts_t")
        s_s1j = sem("first_parts_j")
        s_pj = sem("p_j_copied")
        s_rest_t = sem("rests_t_ready")
        s_rest_j = sem("rests_j_ready")
        s_p23 = sem("parts_ready")
        s_pt = sem("second_parts_t")
        s_pjj = sem("second_parts_j")
        s_f23 = sem("f_parts_ready")
        s_fed = [sem(f"z_operands_loaded{i}") for i in range(2)]
        s_hmt = sem("hm_t_psum")
        s_hmc = sem("hm_t_copied")
        s_y = sem("edge_out_psum")
        s_x2 = sem("x2_ready")
        s_edge0 = sem("edge_phase_prepared")
        s_count = sem("counts_times_p")
        s_sum_q = sem("parts_summed")
        s_bn = sem("bn_vector")
        s_deg = sem("degree_square_roots")
        s_bnp = sem("bn_psum")
        s_bna = sem("bn_scalar")
        L = Points("p2", vector=("a_used", "y_ready", "xc", "v", "h3_ready", "max_ready",
                                 "att_scaled", "out_ready"),
                   scalar=("h2_ready", "at_copied", "dt_copied", "sq", "log", "root", "h3t_copied", "terms_copied", "wh_copied", "e_copied", "exp_done", "pt_copied",
                           "elu_exp"),
                   tensor=("at_psum", "dt_psum", "x_psum", "ay_psum", "h3t_psum", "wh_psum", "e_psum", "pt_psum",
                           "att_psum"))
        L_steps = [sem(f"p2_vector_steps{u}") for u in range(U)]
        s_sum = sem("norm_differences")
        s_sq = sem("norm_squares")
        s_root = sem("norm_roots")
        s_var = sem("norm_variances")
        s_vn = sem("norm_steps")
        s_out = [sem(f"out_stored{u}") for u in range(U)]
        s_out_free = [sem(f"out_tile_free{u}") for u in range(U)]
        s_a2 = [sem(f"adj_loaded_again{u}") for u in range(U)]

        block = ctx.enter_context(nc.Block())

        def own_steps(eng, s, start, per_round=0, rnd=0):
            done = [0]

            def step(ins):
                done[0] += 1
                ins.then_inc(s, 1)
                eng.wait_ge(s, start + per_round * rnd + done[0])
            step.done = done
            return step

        def position(n):
            a, o = n // 2, n % 2
            return HB * (a + 8 * o) if a < 8 else 2 * OH + HB * (a - 8 + 4 * o)

        def starts_anew(n):
            return n % 2 == 0 or n < 4

        def in_turn(*programs):
            programs = list(programs)
            while programs:
                programs = [p for p in programs if next(p, self_done) is not self_done]

        self_done = object()

        def nothing(u, t):
            yield

        def stages_in_turn(eng, stages):
            for k in range(U):
                in_turn(*(stages[k - u](u, 0) for u in range(k + 1)))
            with eng.Fori(1, ROUNDS) as t:
                for k in range(U):
                    in_turn(*(stages[(k - u) % U](u, t if u <= k else t - 1) for u in range(U)))
            for k in range(U - 1):
                in_turn(*(stages[(k - u) % U](u, ROUNDS - 1) for u in range(k + 1, U)))

        def pieces(n):
            for _ in range(n):
                yield

        def piecewise(eng, s, per_round, t, first=0):
            done = [first]

            def step(ins):
                done[0] += 1
                ins.then_inc(s, 1)
                yield
                eng.wait_ge(s, t * per_round + done[0])
            step.done = done
            return step

        adj_v = adj_d.rearrange("(g b) i k -> g i b k", b=GB)
        out_v = out_d.rearrange("(g b) j f -> g j b f", b=GB)

        W_LOADS = 13
        V_LN = 7
        V_P0 = 2 * V_LN + 7
        V_AY = 3
        V_VAR = V_AY + 6
        V_H3 = V_VAR + 3
        V_P2 = V_H3 + 5

        @block.sync
        def _(sp):
            x_v = x_d.rearrange("b j f -> j b f")
            nb = B // ROUNDS
            for c in range(ROUNDS):
                sp.dma_start(x_all[:, 1 + c * nb:1 + (c + 1) * nb, :], x_v[:, c * nb:(c + 1) * nb, :]).then_inc(s_x, 16)
                if c == 0:
                    for u in range(U):
                        sp.dma_start(abuf[u][:], adj_v[u]).then_inc(s_a[u], 16)
                    weights = [(b2_bc[:], b2_d.rearrange("(o f) -> o f", o=1).broadcast_to([N, D])),
                               (w2[:], w2_d.rearrange("(c h) o -> h c o", c=2)),
                               (b3_bc[:], b3_d.rearrange("(o f) -> o f", o=1).broadcast_to([N, D])),
                               (a_c[:, 0:1], a_d[0:D, :]), (a_c[:, 1:2], a_d[D:2 * D, :])]
                    for half in (slice(0, D), slice(D, 2 * D)):
                        weights += [(gamma_c[half], gamma_d.rearrange("(f o) -> f o", o=1)),
                                    (beta_c[half], beta_d.rearrange("(f o) -> f o", o=1)), (w3[half], w3_d), (w4[half], w4_d)]
                    assert len(weights) == W_LOADS
                    for dst, src in weights:
                        sp.dma_start(dst, src).then_inc(s_w, 16)
                sp.wait_ge(s_x, c * 16 + 16)
            with sp.Fori(0, ROUNDS - 1) as t:
                for u in range(U):
                    sp.wait_ge(A.sem("a_used", u), A.now("a_used", t))
                    sp.dma_start(abuf[u][:], adj_v[bass.ds((t + 1) * U + u, 1)].rearrange("o i b k -> (o i) b k")).then_inc(s_a[u], 16)

            def feed(m, half):
                sp.wait_ge(s_zfree_lq, m + 1)
                sp.wait_ge(s_p23, m + 1)
                for c in range(3):
                    for n in range(NOH - 1):
                        sp.dma_start(lq[half][OH * c:OH * (c + 1), n, :],
                                     parts[half][OH * n:OH * (n + 1), c, 1, :]).then_inc(s_fed[half], 16)
                sp.wait_ge(s_zfree, m + 1)
                n = NOH - 1
                for c in range(3):
                    sp.dma_start(rhs[half][3 * OH + c:3 * OH + c + 1, :, :], parts[half][:, c, 0, :]).then_inc(s_fed[half], 16)
                    sp.dma_start(lq[half][OH * c:OH * (c + 1), n, :],
                                 parts[half][OH * n:OH * (n + 1), c, 1, :]).then_inc(s_fed[half], 16)

            sp.wait_ge(s_const, 1)
            feed(0, 0)
            feed(1, 1)
            with sp.Fori(0, B // 2) as pair:
                for b in (pair * 2, pair * 2 + 1):
                    for half in range(2):
                        feed(b * 2 + half + 2, half)

            for u in range(U):
                sp.wait_ge(A.sem("a_used", u), A.before("a_used", ROUNDS))
                sp.dma_start(abuf[u][:], adj_v[u]).then_inc(s_a2[u], 16)

            def store(gi, u, t):
                sp.wait_ge(L.sem("out_ready", u), L.now("out_ready", t))
                sp.dma_start(out_v[bass.ds(gi, 1)].rearrange("o j b f -> (o j) b f"), outb[u]).then_inc(s_out[u], 16)
                sp.wait_ge(s_out[u], t * 16 + 16)
                sp.sem_inc(s_out_free[u], 1)

            for u in range(U):
                sp.sem_inc(s_out_free[u], 1)
            def load_again(u, t):
                sp.wait_ge(L.sem("a_used", u), L.now("a_used", t))
                sp.dma_start(abuf[u][:], adj_v[bass.ds((t + 1) * U + u, 1)].rearrange("o i b k -> (o i) b k")).then_inc(s_a2[u], 16)

            with sp.Fori(0, ROUNDS - 1) as t:
                for u in range(U):
                    load_again(u, t)
                for u in range(U):
                    store(t * U + u, u, t)
            for u in range(U):
                store(NG - U + u, u, ROUNDS - 1)
            for u in range(U):
                sp.wait_ge(s_out[u], 16 * ROUNDS)

        @block.gpsimd
        def _(pool):
            step = own_steps(pool, s_pool, 0)
            gp = nc.gpsimd
            step(gp.memset(ident[:], 0.0))
            gp.affine_select(out=ident[:], in_=ident[:], compare_op=ALU.not_equal, fill=1.0, base=0,
                             pattern=[[-1, N]], channel_multiplier=1).then_inc(s_ident, 1)
            pool.wait_ge(s_ident, 1)
            step(gp.memset(negbig_ident[:], 0.0))
            step(gp.affine_select(out=negbig_ident[:], in_=negbig_ident[:], compare_op=ALU.not_equal, fill=-BIG, base=0,
                                  pattern=[[-1, N]], channel_multiplier=1))
            step(gp.memset(ones_bf[:], 1.0))
            for i in range(2):
                step(gp.memset(rhs[i][:], 0.0))
                for c in range(3):
                    v = rhs[i][OH * c:OH * (c + 1)].rearrange("p (n h) j -> p n h j", h=OH)
                    step(gp.affine_select(out=v, in_=v, compare_op=ALU.not_equal, fill=1.0, base=0,
                                          pattern=[[0, NOH], [-1, OH], [0, N]], channel_multiplier=1))
                step(gp.memset(lq[i][3 * OH:], 1.0))
            step(gp.memset(ones_f[:], 1.0))
            step(gp.memset(h_t_all[D:D + 1, :, :], 1.0))
            step(gp.memset(h_t_all[0:D, B, :], 0.0))
            step(gp.memset(hm[:], 0.0))
            for i in range(8 - LAG, 8):
                step(gp.memset(g[i][:], 0.0))
            step(gp.memset(f4[1][:, :, 1:4], 0.0))
            gp.memset(x_all[:, 0, :], 0.0).then_inc(s_const, 1)

            def later_parts_t(m, half):
                pool.wait_ge(s_rest_t, m + 1)
                gp.tensor_tensor(wait_carrier[:], ones_f[:, 0:1], ones_f[:, 0:1], ALU.mult)
                gp.tensor_copy(parts[half][:, 1], rest_t[:]).then_inc(s_pt, 1)
                pool.wait_ge(s_pt, m + 1)
                gp.tensor_tensor(parts[half][:, 2], rest_t[:], parts[half][:, 1], ALU.subtract).then_inc(s_p23, 1)

            def later_parts_j(m, half):
                pool.wait_ge(s_rest_j, m + 1)
                gp.tensor_tensor(wait_carrier[:], ones_f[:, 0:1], ones_f[:, 0:1], ALU.mult)
                gp.tensor_copy(f4[half][:, :, 2], rest_j[:]).then_inc(s_pjj, 1)
                pool.wait_ge(s_pjj, m + 1)
                gp.tensor_tensor(f4[half][:, :, 3], rest_j[:], f4[half][:, :, 2], ALU.subtract).then_inc(s_f23, 1)

            pool.wait_ge(s_const, 1)
            later_parts_t(0, 0)
            later_parts_t(1, 1)
            later_parts_j(0, 0)
            with pool.Fori(0, B // 2) as pair:
                for b in (pair * 2, pair * 2 + 1):
                    for half in range(2):
                        later_parts_t(b * 2 + half + 2, half)
                        later_parts_j(b * 2 + half + 1, 1 - half)

        @block.scalar
        def _(act):
            sc = nc.scalar

            for dst, src in ((w1a[:], w1_d[0:D, :]), (w1b[:], w1_d[D:2 * D, :]),
                             (w_j[D:D + 1, :, 0, :], b1_d.rearrange("(o c h) -> o c h", o=1, c=2))):
                act.dma_start(dst, src).then_inc(s_w1, 16)

            def flat(tile):
                return tile.rearrange("p b k -> p (b k)")

            act.sem_inc(s_ga, 2)
            A.start(act, "at_copied")
            L.start(act, "at_copied")

            def first_norm(u, t):
                act.wait_ge(A.sem("edges_ready", u), A.before("edges_ready", t))
                act.wait_ge(A.sem("at_psum", u), A.now("at_psum", t))
                sc.copy(flat(a_t[u][:]), bank[2 * u][:]).then_inc(A.sem("at_copied", u), 1)
                yield
                yield from norm(u, t, "1")

            def norm(u, t, k):
                act.wait_ge(A.sem("xc" + k, u), A.now("xc" + k, t))
                sc.square(sq[u][:], xc[u][:]).then_inc(A.sem("sq" + k, u), 1)
                yield
                act.wait_ge(A.sem("v" + k, u), A.now("v" + k, t))
                sc.sqrt(stat[u][:, 3, :], stat[u][:, 2, :]).then_inc(A.sem("root" + k, u), 1)
                yield

            def aggregate(u, t):
                for _ in range(3):
                    yield
                yield from norm(u, t, "2")
                act.wait_ge(A.sem("h1t_psum", u), A.now("h1t_psum", t))
                sc.copy(h_t_all[0:D, bass.ds((t * U + u) * GB, GB), :],
                        bank[2 * u][0:D, :].rearrange("p (b k) -> p b k", b=GB)).then_inc(A.sem("h1t_copied", u), 1)
                yield

            in_turn(first_norm(0, 0), first_norm(1, 0))
            in_turn(first_norm(2, 0), first_norm(3, 0), aggregate(0, 0), aggregate(1, 0))
            with act.Fori(1, ROUNDS) as t:
                in_turn(first_norm(0, t), first_norm(1, t), aggregate(2, t - 1), aggregate(3, t - 1))
                in_turn(first_norm(2, t), first_norm(3, t), aggregate(0, t), aggregate(1, t))
            in_turn(aggregate(2, ROUNDS - 1), aggregate(3, ROUNDS - 1))

            def copy_h_t(m, gb):
                act.wait_ge(s_pqj, m)
                sc.square(act_wait_carrier[:], ones_f[:, 0:1])
                sc.copy(h_t[:], h_t_all[:, gb, :]).then_inc(s_ht, 1)

            def first_parts_t(m, half, loaded):
                act.wait_ge(s_ptq, m + 1)
                if loaded is not None:
                    act.wait_ge(s_fed[half], loaded)
                sc.copy(parts[half][:, 0].rearrange("p a b -> p (a b)"), bank[6][0:HALF, 0:2 * N]).then_inc(s_s1t, 1)

            def first_parts_j(m, half, combined):
                act.wait_ge(s_pqj, m + 1)
                if combined is not None:
                    act.wait_ge(s_f23, m)
                sc.copy(f4[half][:, :, 1], bank[7][:, HALF:2 * HALF]).then_inc(s_s1j, 1)
                if combined is not None:
                    act.wait_ge(s_comb[half], combined)
                sc.copy(p_j[half][:], bank[7][:, 0:HALF]).then_inc(s_pj, 1)

            def copy_hm_t(done):
                act.wait_ge(s_hmt, done)
                sc.copy(hm_t[:].rearrange("p c j -> p (c j)"), bank[6][0:HALF, 2 * N:4 * N]).then_inc(s_hmc, 1)

            act.wait_ge(s_p0, 1)
            act.wait_ge(s_const, 1)
            for u in range(U):
                act.wait_ge(A.sem("h1t_copied", u), A.before("h1t_copied", ROUNDS))
            sc.copy(h_t[:], h_t_all[:, 0, :]).then_inc(s_ht, 1)
            for m in range(2):
                first_parts_t(m, m, None)
            first_parts_j(0, 0, None)
            with act.Fori(0, B // 2) as pair:
                for b in (pair * 2, pair * 2 + 1):
                    for n in range(2 * QB):
                        half, q = n // QB, n % QB
                        if q == 2:
                            copy_h_t(b * 2 + half + 1, bass.ds(b + half, 1))
                        if q == 5:
                            first_parts_t(b * 2 + half + 2, half, (b + 1) * 16 * 12)
                        if q == 11:
                            first_parts_j(b * 2 + half + 1, 1 - half, b + 1 + half)
                        if n == 15:
                            copy_hm_t(b + 1)
                        if n % 2:
                            act.wait_ge(s_za, b * QB + n // 2 + 1)
                            sc.activation(g[n % 8][:].rearrange("p h j -> p (h j)"), bank[n % 4][:], ACT.Sign).then_inc(s_ga, 1)
            copy_hm_t(B + 1)

            sc.sqrt(norm_stat[:, 3, :], degrees[:]).then_inc(s_deg, 1)
            for c in range(4):
                act.wait_ge(s_sum, c + 1)
                sc.square(scratch[1][:, c * 1024:(c + 1) * 1024], scratch[0][:, c * 1024:(c + 1) * 1024]).then_inc(s_sq, 1)
            act.wait_ge(s_var, 1)
            sc.sqrt(norm_stat[:, 3, :], norm_stat[:, 2, :]).then_inc(s_root, 1)
            for c in range(4):
                act.wait_ge(s_sum, 4 + c + 1)
                sc.square(scratch[1][:, c * 1024:(c + 1) * 1024], scratch[0][:, c * 1024:(c + 1) * 1024]).then_inc(s_sq, 1)
            act.wait_ge(s_bn, 4)
            sc.activation(bn_v[:, 1:2], bn_v[:, 0:1], ACT.Sqrt).then_inc(s_bna, 1)

            def aggregate_2(u, t):
                act.wait_ge(L.sem("h3t_psum", u), L.before("h3t_psum", t))
                sc.copy(h2_h3[u], h2_all[:, bass.ds((t * U + u) * GB, GB), :]).then_inc(L.sem("h2_ready", u), 1)
                act.wait_ge(L.sem("at_psum", u), L.now("at_psum", t))
                sc.copy(flat(a_t[u][:]), bank[2 * u][:]).then_inc(L.sem("at_copied", u), 1)
                yield
                act.wait_ge(L.sem("dt_psum", u), L.now("dt_psum", t))
                sc.copy(flat(h2_t[u]), bank[2 * u + 1][:, 0:2 * N]).then_inc(L.sem("dt_copied", u), 1)

            def residual_norm(u, t):
                yield from pieces(7)
                act.wait_ge(L.sem("xc", u), L.now("xc", t))
                sc.square(sq[u][:], xc[u][:]).then_inc(L.sem("sq", u), 1)
                yield from pieces(3)
                act.wait_ge(L.sem("v", u), L.now("v", t))
                sc.activation(stat[u][:, 3, :], stat[u][:, 2, :], ACT.Ln).then_inc(L.sem("log", u), 1)
                yield
                act.wait_ge(L.sem("log", u), L.now("log", t))
                sc.activation(stat[u][:, 4, :], stat[u][:, 3, :], ACT.Exp, scale=-0.5).then_inc(L.sem("root", u), 1)

            def attention_logits(u, t):
                yield from pieces(5)
                act.wait_ge(L.sem("h3t_psum", u), L.now("h3t_psum", t))
                sc.copy(flat(h3_t[u]), bank[2 * u][:, 0:2 * N]).then_inc(L.sem("h3t_copied", u), 1)
                yield from pieces(3)
                act.wait_ge(L.sem("wh_psum", u), L.now("wh_psum", t))
                products = bank[2 * u + 1][:, 0:GB * (D + 2)].rearrange("p (b f) -> p b f", b=GB)
                sc.copy(terms[u][:], products[:, :, D:D + 2]).then_inc(L.sem("terms_copied", u), 1)
                sc.copy(wh[u], products[:, :, 0:D]).then_inc(L.sem("wh_copied", u), 1)
                yield from pieces(3)
                act.wait_ge(L.sem("terms_copied", u), L.now("terms_copied", t))
                act.wait_ge(L.sem("e_psum", u), L.now("e_psum", t))
                for i in range(GB):
                    last = sc.activation(pairs[u][:, i, :], bank[2 * u][:, N * i:N * (i + 1)], ACT.Identity,
                                         bias=terms[u][:, i, 0:1])
                last.then_inc(L.sem("e_copied", u), 1)

            def attention_sums(u, t):
                yield from pieces(3)
                act.wait_ge(L.sem("max_ready", u), L.now("max_ready", t))
                for i in range(GB):
                    last = sc.activation(pairs[u][:, i, :], no_edge[u][:, i, :], ACT.Exp, bias=stat[u][:, 9, i:i + 1],
                                         accum_out=stat[u][:, 10, i:i + 1])
                last.then_inc(L.sem("exp_done", u), 1)
                yield from pieces(3)
                act.wait_ge(L.sem("pt_psum", u), L.now("pt_psum", t))
                sc.copy(flat(probs_t[u]), bank[2 * u + 1][:]).then_inc(L.sem("pt_copied", u), 1)
                yield from pieces(5)
                act.wait_ge(L.sem("att_scaled", u), L.now("att_scaled", t))
                sc.activation(yl[u], tmp[u][:], ACT.Exp).then_inc(L.sem("elu_exp", u), 1)

            stages_in_turn(act, (aggregate_2, residual_norm, attention_logits, attention_sums))

        @block.tensor
        def _(pe):
            te = nc.tensor

            A.start(pe, "at_psum")
            L.start(pe, "at_psum")

            def first_norm(u, t):
                pe.wait_ge(A.sem("h1t_copied", u), A.before("h1t_copied", t))
                pe.wait_ge(s_a[u], t * 16 + 16)
                for i in range(GB):
                    last = te.transpose(bank[2 * u][:, N * i:N * (i + 1)], abuf[u][:, i, :], ident[:])
                last.then_inc(A.sem("at_psum", u), 1)
                yield
                pe.wait_ge(A.sem("edges_ready", u), A.now("edges_ready", t))
                pe.wait_ge(A.sem("at_copied", u), A.now("at_copied", t))
                for i in range(GB):
                    te.matmul(bank[2 * u + 1][:, (D + 1) * i:(D + 1) * (i + 1)], a_t[u][:, i, :], hn[u][:, i, :],
                              start=True, stop=True)
                for i in range(GB):
                    last = te.matmul(bank[2 * u + 1][:, (D + 1) * GB + i:(D + 1) * GB + i + 1],
                                     edge_t_all[:, bass.ds((t * U + u) * GB + i, 1), :].rearrange("p o k -> p (o k)"),
                                     ones_col[:], start=True, stop=True)
                last.then_inc(A.sem("l0_psum", u), 1)
                yield

            def aggregate(u, t):
                for _ in range(2):
                    yield
                pe.wait_ge(A.sem("h1_ready", u), A.now("h1_ready", t))
                te.matmul(bank[2 * u][:, 511:512], ident[:], ident[:, 0:1], start=True, stop=True)
                for i in range(GB):
                    last = te.transpose(bank[2 * u][0:D, N * i:N * (i + 1)], hn[u][:, i, 0:D], ident[:])
                last.then_inc(A.sem("h1t_psum", u), 1)
                yield

            pe.wait_ge(s_ident, 1)
            pe.wait_ge(s_ones, 1)
            in_turn(first_norm(0, 0), first_norm(1, 0))
            in_turn(first_norm(2, 0), first_norm(3, 0), aggregate(0, 0), aggregate(1, 0))
            with pe.Fori(1, ROUNDS) as t:
                in_turn(first_norm(0, t), first_norm(1, t), aggregate(2, t - 1), aggregate(3, t - 1))
                in_turn(first_norm(2, t), first_norm(3, t), aggregate(0, t), aggregate(1, t))
            in_turn(aggregate(2, ROUNDS - 1), aggregate(3, ROUNDS - 1))

            pe.wait_ge(s_const, 1)
            pe.wait_ge(s_w, 16 * W_LOADS)
            for u in range(U):
                pe.wait_ge(A.sem("h1t_copied", u), A.before("h1t_copied", ROUNDS))
            te.transpose(bank[0][0:D, 0:D], w4[0:D, :], ident[0:D, 0:D]).then_inc(s_bnp, 1)
            pe.wait_ge(s_wprep, 1)
            te.matmul(bank[0][:, 64:66], w4_t[:].rearrange("p o f -> p (o f)"), a_c[:], start=True, stop=True).then_inc(s_bnp, 1)
            pe.wait_ge(s_wprep, 2)

            def project_t(m, half, gb):
                if m is not None:
                    pe.wait_ge(s_rest_t, m)
                for k in range(2):
                    last = te.matmul(bank[6][0:HALF, N * k:N * (k + 1)], w_t[:, half, k, :], h_t_all[:, gb, :],
                                     start=True, stop=True)
                last.then_inc(s_ptq, 1)

            def project_j(m, half):
                pe.wait_ge(s_ht, m + 1)
                te.matmul(bank[7][:, 0:2 * HALF], h_t[:], w_j[:, half].rearrange("p a b -> p (a b)"),
                          start=True, stop=True).then_inc(s_pqj, 1)

            def edge_out_t(done, rests):
                pe.wait_ge(s_comb[1], done)
                pe.wait_ge(s_rest_t, rests)
                for k in range(2):
                    last = te.transpose(bank[6][0:HALF, 2 * N + N * k:2 * N + N * (k + 1)], hm[:, k, :], ident[:])
                last.then_inc(s_hmt, 1)

            def edge_out(done, rests):
                pe.wait_ge(s_hmc, done)
                pe.wait_ge(s_rest_j, rests)
                for k in range(2):
                    last = te.matmul(bank[7][:, 2 * HALF:2 * HALF + D], hm_t[:, k, :], w2[:, k, :], start=(k == 0), stop=(k == 1))
                last.then_inc(s_y, 1)

            pe.wait_ge(s_edge0, 1)
            pe.sem_inc(s_zfree_lq, 2)
            pe.sem_inc(s_zfree, 2)
            for m in range(2):
                project_t(m if m else None, m, 0)
            project_j(0, 0)
            with pe.Fori(0, B // 2) as pair:
                for b in (pair * 2, pair * 2 + 1):
                    def masked_sum(n, rnd):
                        half, q = n // QB, n % QB
                        if q == 0:
                            pe.wait_ge(s_comb[half], rnd + 1)
                            pe.wait_ge(s_f23, rnd * 2 + half + 1)
                            te.matmul(bank[4 + half][:, 0:4 * HALF].rearrange("p (a o c) -> p a o c", o=2, c=4 * HB)[:, :, 1, :],
                                      ones_bf[:],
                                      f4[half][:].rearrange("p (a o h) c -> p a o (h c)", o=2, h=HB)[:, :, 1, :],
                                      start=True, stop=True, skip_group_check=True)
                        pe.wait_ge(s_ga if n % 2 else s_gd, rnd * QB + n // 2 + 3)
                        for i in range(HB):
                            h = q * HB + i
                            last = te.matmul(bank[4 + half][:, 4 * h:4 * h + 4], g[n % 8][:, i, :], f4[half][:, h, :],
                                             start=False, stop=True, skip_group_check=True)
                        if q == QB - 1:
                            last.then_inc(s_r[half], 1)
                        if q == 2 * OH // HB - 1 - LAG:
                            last.then_inc(s_zfree_lq, 1)
                        if q == QB - 1 - LAG:
                            last.then_inc(s_zfree, 1)

                    for n in range(2 * QB):
                        half, q = n // QB, n % QB
                        if q == 2:
                            if half:
                                pe.wait_ge(s_hmc, b + 1)
                            project_t(b * 2 + half + 2, half, bass.ds(b + 1, 1))
                        if q == 5:
                            pe.wait_ge(s_rest_j, b * 2 + half + 1)
                            if half:
                                pe.wait_ge(s_x2, b + 1)
                            project_j(b * 2 + half + 1, 1 - half)
                        if n == 15:
                            edge_out_t(b + 1, b * 2 + 3)
                        if n == 23:
                            edge_out(b + 1, b * 2 + 2)
                        if q == 0:
                            pe.wait_ge(s_fed[half], b * 16 * 12 + 16 * 12)
                        pe.wait_ge(s_ga if n % 2 else s_gd, b * QB + n // 2 + 1)
                        anew = starts_anew(n)
                        at = position(q)
                        last = te.matmul(bank[n % 4][:], lq[half][:, at // OH, :],
                                         rhs[half][:, at:at + HB, :].rearrange("p h j -> p (h j)"),
                                         start=anew, stop=not (n % 2 and anew), skip_group_check=True)
                        if n % 2 and anew:
                            te.matmul(bank[n % 4][:].rearrange("p (h j) -> p h j", h=HB), negbig_ident[:],
                                      no_edge_t_all[:, bass.ds(b, 1), :].broadcast_to([N, HB, N]),
                                      start=False, stop=True, skip_group_check=True).then_inc(s_za, 1)
                        else:
                            last.then_inc(s_za if n % 2 else s_zd, 1)
                        if n >= LAG:
                            masked_sum(n - LAG, b)
                        else:
                            masked_sum(n - LAG + 2 * QB, b - 1)
            for n in range(2 * QB - LAG, 2 * QB):
                masked_sum(n, B - 1)
            edge_out_t(B + 1, 2 * B + 2)
            edge_out(B + 1, 2 * B + 1)

            pe.wait_ge(s_bn, 1)
            sums = bn_part[:].rearrange("p o f -> p (o f)")
            te.matmul(bank[0][:, 0:D], ones_f[:], bn_part[:, 0, :], start=True, stop=True)
            te.matmul(bank[0][:, 64:65], sums, ones_f[:, 0:1], start=True, stop=True).then_inc(s_bnp, 1)
            pe.wait_ge(s_bn, 3)
            te.matmul(bank[0][:, 64:65], sums, ones_f[:, 0:1], start=True, stop=True).then_inc(s_bnp, 1)
            pe.wait_ge(s_bn, 5)
            te.matmul(bank[1][:, 0:D], shift_bc[:], w3[0:D, :], start=True, stop=True).then_inc(s_bnp, 1)
            pe.wait_ge(s_bn, 6)

            def aggregate_2(u, t):
                pe.wait_ge(L.sem("att_scaled", u), L.before("att_scaled", t))
                pe.wait_ge(s_a2[u], t * 16 + 16)
                for i in range(GB):
                    last = te.transpose(bank[2 * u][:, N * i:N * (i + 1)], abuf[u][:, i, :], ident[:])
                last.then_inc(L.sem("at_psum", u), 1)
                yield
                pe.wait_ge(L.sem("pt_copied", u), L.before("pt_copied", t))
                pe.wait_ge(L.sem("h2_ready", u), L.now("h2_ready", t))
                te.matmul(bank[2 * u + 1][:, 511:512], ident[:], ones_f[:, 0:1], start=True, stop=True)
                for i in range(GB // 2):
                    last = te.transpose(bank[2 * u + 1][:, N * i:N * (i + 1)],
                                        h2_h3[u][:, 2 * i:2 * i + 2, :].rearrange("p o f -> p (o f)"), ident[:])
                last.then_inc(L.sem("dt_psum", u), 1)
                yield from pieces(4)
                pe.wait_ge(L.sem("at_copied", u), L.now("at_copied", t))
                pe.wait_ge(L.sem("dt_copied", u), L.now("dt_copied", t))
                for i in range(GB // 2):
                    last = te.matmul(bank[2 * u][:, 2 * D * i:2 * D * (i + 1)], h2_t[u][:, i, :],
                                     ws3_pair[:].rearrange("p o f -> p (o f)"), start=True, stop=True)
                last.then_inc(L.sem("x_psum", u), 1)
                yield from pieces(6)
                pe.wait_ge(L.sem("y_ready", u), L.now("y_ready", t))
                for i in range(GB):
                    last = te.matmul(bank[2 * u + 1][:, D * i:D * (i + 1)], a_t[u][:, i, :], yl[u][:, i, :], start=True, stop=True)
                last.then_inc(L.sem("ay_psum", u), 1)

            def attention_logits(u, t):
                yield from pieces(4)
                pe.wait_ge(L.sem("h3_ready", u), L.now("h3_ready", t))
                te.matmul(bank[2 * u][:, 511:512], ident[:], ones_f[:, 0:1], start=True, stop=True)
                for i in range(GB // 2):
                    last = te.transpose(bank[2 * u][:, N * i:N * (i + 1)],
                                        h2_h3[u][:, 2 * i:2 * i + 2, :].rearrange("p o f -> p (o f)"), ident[:])
                last.then_inc(L.sem("h3t_psum", u), 1)
                yield from pieces(2)
                pe.wait_ge(L.sem("h3t_copied", u), L.now("h3t_copied", t))
                for i in range(GB // 2):
                    last = te.matmul(bank[2 * u + 1][:, 2 * (D + 2) * i:2 * (D + 2) * (i + 1)], h3_t[u][:, i, :],
                                     w4_pair[:].rearrange("p o f -> p (o f)"), start=True, stop=True)
                last.then_inc(L.sem("wh_psum", u), 1)
                yield from pieces(3)
                pe.wait_ge(L.sem("terms_copied", u), L.now("terms_copied", t))
                for i in range(GB):
                    last = te.transpose(bank[2 * u][:, N * i:N * (i + 1)], terms[u][:, i, 1:2].broadcast_to([N, N]), ident[:])
                last.then_inc(L.sem("e_psum", u), 1)

            def attention_sums(u, t):
                yield from pieces(5)
                pe.wait_ge(L.sem("exp_done", u), L.now("exp_done", t))
                for i in range(GB):
                    last = te.transpose(bank[2 * u + 1][:, N * i:N * (i + 1)], pairs[u][:, i, :], ident[:])
                last.then_inc(L.sem("pt_psum", u), 1)
                yield from pieces(2)
                pe.wait_ge(L.sem("pt_copied", u), L.now("pt_copied", t))
                for i in range(GB):
                    last = te.matmul(bank[2 * u][:, D * i:D * (i + 1)], probs_t[u][:, i, :], wh[u][:, i, :], start=True, stop=True)
                last.then_inc(L.sem("att_psum", u), 1)
                yield

            stages_in_turn(pe, (aggregate_2, nothing, attention_logits, attention_sums))

        @block.vector
        def _(dve):
            ve = nc.vector

            def bc(col, n=D, m=GB):
                return col.rearrange("p (b o) -> p b o", o=1).broadcast_to([N, m, n])

            def inverse_root(step, v, root, r, t, u, out):
                yield from step(ve.reciprocal(r, root))
                yield from newton(step, v, r, t, u, out)

            def newton(step, v, r, t, u, out):
                yield from step(ve.tensor_tensor(t, r, r, ALU.mult))
                yield from step(ve.scalar_tensor_tensor(out=u, in0=t, scalar=-0.5, in1=v, op0=ALU.mult, op1=ALU.mult))
                yield from step(ve.scalar_tensor_tensor(out=out, in0=u, scalar=1.5, in1=r, op0=ALU.add, op1=ALU.mult))

            def variance(step, x, u, t, points, k, idle=0):
                st = stat[u]
                ve.memset(st[:, 11, :], 0.0)
                yield from step(ve.tensor_reduce(st[:, 0, :], x, AX_X, ALU.add))
                yield from step(ve.tensor_scalar(st[:, 1, :], st[:, 0, :], 1.0 / D, None, ALU.mult))
                ve.tensor_tensor(xc[u][:], x, bc(st[:, 1, :]), ALU.subtract).then_inc(points.sem("xc" + k, u), 1)
                yield from pieces(1 + idle)
                dve.wait_ge(points.sem("sq" + k, u), points.now("sq" + k, t))
                yield from step(ve.tensor_reduce(st[:, 0, :], sq[u][:], AX_X, ALU.add))
                ve.tensor_scalar(st[:, 2, :], st[:, 0, :], 1.0 / D, LN_EPS, ALU.mult, ALU.add).then_inc(points.sem("v" + k, u), 1)

            def relu_scaled(out, u):
                return ve.scalar_tensor_tensor(out=out, in0=xc[u][:], scalar=0.0, in1=bc(stat[u][:, 7, :]),
                                               op0=ALU.max, op1=ALU.mult)

            def norm_relu(step, x, out, u, t, points, k, done):
                st = stat[u]
                yield from variance(step, x, u, t, points, k)
                yield
                dve.wait_ge(points.sem("v" + k, u), points.now("v" + k, t))
                dve.wait_ge(points.sem("root" + k, u), points.now("root" + k, t))
                yield from inverse_root(step, st[:, 2, :], st[:, 3, :], st[:, 4, :], st[:, 5, :], st[:, 6, :], st[:, 7, :])
                relu_scaled(out, u).then_inc(points.sem(done, u), 1)

            def whole(program):
                for _ in program:
                    pass

            def waiting(step):
                def run(ins):
                    step(ins)
                    return iter(())
                return run

            A.start(dve, "xc1")
            L.start(dve, "a_used")
            dve.sem_inc(s_comb[0], 1)
            dve.sem_inc(s_gd, 2)
            for u in range(U):
                ve.memset(hn[u][:, :, D:D + 1], 1.0)
            ve.memset(ones_col[:], 1.0).then_inc(s_ones, 1)
            step = own_steps(dve, s_dve, 0)
            dve.wait_ge(s_w1, 16 * 3)
            wa = w1a[:].rearrange("p (c h) -> p c h", c=2)
            wb = w1b[:].rearrange("p (c h) -> p c h", c=2)
            ve.memset(w_j[D:D + 1, :, 1, :], 0.0)
            ve.tensor_tensor(w_j[0:D, :, 0, :], wa, wb, ALU.add)
            step(ve.tensor_scalar(w_j[0:D, :, 1, :], wb, -1.0, None, ALU.mult))
            for c in range(2):
                by_block, before = (w_j[:, i].rearrange("p k (a o h) -> p k a o h", o=2, h=HB) for i in (c, 0))
                for first, count in ((0, 8), (8, 4)):
                    at, at_odd = position(2 * first), position(2 * first + 1)
                    end = first + count
                    for k in range(2):
                        run = w_t[:, c, k, at:at + HB * count].rearrange("p (a h) -> p a h", h=HB)
                        ve.tensor_copy(run, by_block[:, k, first:end, 0])
                        run = w_t[:, c, k, at_odd:at_odd + HB * count].rearrange("p (a h) -> p a h", h=HB)
                        odd = by_block[:, k, :, 1]
                        if first:
                            ve.tensor_tensor(run, odd[:, first:end], odd[:, first - 2:end - 2], ALU.subtract)
                        else:
                            ve.tensor_tensor(run[:, 2:], odd[:, 2:end], odd[:, :end - 2], ALU.subtract)
                            if c:
                                ve.tensor_tensor(run[:, 0:2], odd[:, 0:2], before[:, k, -2:, 1], ALU.subtract)
                            else:
                                ve.tensor_copy(run[:, 0:2], odd[:, 0:2])
            step(ve.memset(p_j[0][:], 0.0))
            for c in range(2):
                halved = w_j[:, c, 1, :].rearrange("p (a o h) -> p a o h", o=2, h=HB)[:, :, 1, :]
                ve.tensor_scalar(halved, halved, 0.5, None, ALU.mult)
                fq = f4[c][:].rearrange("p (a o h) c -> p a o h c", o=2, h=HB)
                ve.memset(fq[:, :, 0, :, 0], 1.0)
                ve.memset(fq[:, :, 1, :, 0], 0.5)
            ve.memset(p_j[1][:], 0.0).then_inc(s_edge0, 1)

            def first_norm(u, t):
                yield from pieces(2)
                step = piecewise(dve, A_steps[u], V_P0, t)
                st = stat[u]
                x = x_all[:, bass.ds((t * U + u) * GB + 1, GB), :]
                if u % 2 == 0:
                    dve.wait_ge(s_x, t * 16 + 16)
                    ve.memset(st[:, 8, :], 0.0)
                dve.wait_ge(A.sem("h1t_psum", u), A.before("h1t_psum", t))
                yield from norm_relu(step, x, hn[u][:, :, 0:D], u, t, A, "1", "h0_ready")
                yield from pieces(2)
                dve.wait_ge(A.sem("at_copied", u), A.now("at_copied", t))
                ve.tensor_scalar(edge_t_all[:, bass.ds((t * U + u) * GB, GB), :], a_t[u][:], 0.0, None, ALU.is_gt)
                ve.tensor_scalar(no_edge_t_all[:, bass.ds((t * U + u) * GB, GB), :], a_t[u][:], 0.0, None, ALU.is_le)\
                    .then_inc(A.sem("edges_ready", u), 1)
                yield
                assert step.done[0] == V_LN, step.done
                yield from pieces(2)

            def aggregate(u, t):
                for _ in range(5):
                    yield
                step = piecewise(dve, A_steps[u], V_P0, t, V_LN)
                st = stat[u]
                x = x_all[:, bass.ds((t * U + u) * GB + 1, GB), :]
                dve.wait_ge(A.sem("l0_psum", u), A.now("l0_psum", t))
                ve.memset(st[:, 11, :], 0.0).then_inc(A.sem("a_used", u), 1)
                sums = bank[2 * u + 1][:, 0:GB * (D + 1)].rearrange("p (b f) -> p b f", b=GB)
                ve.tensor_copy(degrees[:, bass.ds((t * U + u) * GB, GB)], sums[:, :, D])
                yield from step(ve.tensor_scalar(st[:, 10, :], sums[:, :, D], 1.0, None, ALU.max))
                yield from step(ve.reciprocal(st[:, 6, :], st[:, 10, :]))
                yield from step(ve.tensor_tensor(tmp[u][:], sums[:, :, 0:D], bc(st[:, 6, :]), ALU.mult))
                yield from step(ve.tensor_tensor(x, x, tmp[u][:], ALU.add))
                yield from step(ve.tensor_copy(st[:, 10, :], bank[2 * u + 1][:, GB * (D + 1):GB * (D + 2)]))
                yield from norm_relu(step, x, hn[u][:, :, 0:D], u, t, A, "2", "h1_ready")
                yield from step(ve.tensor_tensor(tmp[u][:], b2_bc[:].rearrange("p (o f) -> p o f", o=1).broadcast_to([N, GB, D]),
                                                 bc(st[:, 10, :]), ALU.mult))
                ve.tensor_tensor(x, x, tmp[u][:], ALU.add).then_inc(A_steps[u], 1)
                step.done[0] += 1
                dve.wait_ge(A_steps[u], t * V_P0 + step.done[0])
                assert step.done[0] == V_P0, step.done

            in_turn(first_norm(0, 0), first_norm(1, 0))
            dve.wait_ge(s_w, 16 * W_LOADS)
            in_turn(first_norm(2, 0), first_norm(3, 0), aggregate(0, 0), aggregate(1, 0))
            with dve.Fori(1, ROUNDS) as t:
                in_turn(first_norm(0, t), first_norm(1, t), aggregate(2, t - 1), aggregate(3, t - 1))
                in_turn(first_norm(2, t), first_norm(3, t), aggregate(0, t), aggregate(1, t))
            in_turn(aggregate(2, ROUNDS - 1), aggregate(3, ROUNDS - 1))
            dve.wait_ge(A.sem("h1t_copied", 2), A.before("h1t_copied", ROUNDS))
            for i in (4, 5):
                step(ve.memset(bank[i][:], 0.0))
            ve.memset(stat[0][:, 11, :], 0.0).then_inc(s_p0, 1)
            dve.wait_ge(s_bnp, 1)
            ve.memset(w4_pair[:], 0.0)
            ve.memset(ws3_pair[:], 0.0)
            for k in range(2):
                last = ve.tensor_copy(w4_t[:, k, :], bank[0][0:D, 0:D])
            last.then_inc(s_wprep, 1)
            dve.wait_ge(s_bnp, 2)
            step(ve.tensor_copy(bn_v[:, 0:2], bank[0][:, 64:66]))
            for k, half in enumerate((slice(0, D), slice(D, 2 * D))):
                ve.tensor_copy(w4_pair[half, k, 0:D], w4[half])
                last = ve.tensor_copy(w4_pair[half, k, D:D + 2], bn_v[half, 0:2])
            last.then_inc(s_wprep, 1)

            def rests_t(m, half):
                dve.wait_ge(s_s1t, m + 1)
                if not isinstance(m, int) or m:
                    dve.wait_ge(s_p23, m)
                ve.tensor_tensor(rest_t[:].rearrange("p a b -> p (a b)"), bank[6][0:HALF, 0:2 * N],
                                 parts[half][:, 0].rearrange("p a b -> p (a b)"), ALU.subtract).then_inc(s_rest_t, 1)

            def rests_j(m, half):
                dve.wait_ge(s_s1j, m + 1)
                dve.wait_ge(s_pj, m + 1)
                if not isinstance(m, int) or m:
                    dve.wait_ge(s_f23, m)
                ve.tensor_tensor(rest_j[:], bank[7][:, HALF:2 * HALF], f4[half][:, :, 1], ALU.subtract).then_inc(s_rest_j, 1)

            def sums_of(half):
                return bank[4 + half][:, 0:4 * HALF].rearrange("p (h c) -> p h c", c=4)

            def combine_counts(half):
                ve.tensor_tensor(count_p[:], sums_of(half)[:, :, 0], p_j[half][:], ALU.mult).then_inc(s_count, 1)

            def combine_parts(half, done):
                dve.wait_ge(s_r[half], done)
                ve.tensor_reduce(sum_q[:], sums_of(half)[:, :, 1:4], AX_X, ALU.add).then_inc(s_sum_q, 1)

            def combine(half, done, halves):
                dve.wait_ge(s_count, halves)
                dve.wait_ge(s_sum_q, halves)
                if half == 0:
                    dve.wait_ge(s_hmt, done)
                ve.tensor_tensor(hm[:, half, :], count_p[:], sum_q[:], ALU.add).then_inc(s_comb[half], 1)

            def add_edge_out(slot, done):
                dve.wait_ge(s_y, done)
                x = x_all[:, slot, :]
                ve.tensor_tensor(x, x, bank[7][:, 2 * HALF:2 * HALF + D], ALU.add).then_inc(s_x2, 1)

            dve.wait_ge(s_const, 1)
            for m in range(2):
                rests_t(m, m)
            rests_j(0, 0)
            with dve.Fori(0, B // 2) as pair:
                for b in (pair * 2, pair * 2 + 1):
                    for n in range(2 * QB):
                        half, q = n // QB, n % QB
                        if q == 4:
                            combine_parts(1 - half, b + 1)
                        if q == 5:
                            combine_counts(1 - half)
                        if q == 10:
                            combine(1 - half, b + 1, b * 2 + half + 1)
                        if q == 11:
                            rests_t(b * 2 + half + 2, half)
                        if q == 15:
                            rests_j(b * 2 + half + 1, 1 - half)
                        if n == 23:
                            add_edge_out(bass.ds(b, 1), b + 1)
                        if not n % 2:
                            dve.wait_ge(s_zd, b * QB + n // 2 + 1)
                            ve.scalar_tensor_tensor(out=g[n % 8][:], in0=bank[n % 4][:].rearrange("p (h j) -> p h j", h=HB),
                                                    scalar=0.0, in1=edge_t_all[:, bass.ds(b, 1), :].broadcast_to([N, HB, N]),
                                                    op0=ALU.is_gt, op1=ALU.mult).then_inc(s_gd, 1)
            combine_parts(1, B + 1)
            combine_counts(1)
            combine(1, B + 1, 2 * B + 1)
            add_edge_out(slice(B, B + 1), B + 1)
            dve.wait_ge(s_x2, B + 1)

            for i in range(2):
                dve.wait_ge(s_fed[i], 16 * 12 * (B + 1))
            step = own_steps(dve, s_vn, 0)
            run = waiting(step)
            ns = norm_stat
            quarters = [slice(c * B // 4, (c + 1) * B // 4) for c in range(4)]

            def chunk(i, c):
                return scratch[i][:, c * 1024:(c + 1) * 1024].rearrange("p (b f) -> p b f", f=D)

            for c, qs in enumerate(quarters):
                last = ve.tensor_reduce(ns[:, 0, qs], x_all[:, 1 + qs.start:1 + qs.stop, :], AX_X, ALU.add)
            step(last)
            step(ve.tensor_scalar(ns[:, 1, :], ns[:, 0, :], 1.0 / D, None, ALU.mult))
            for c, qs in enumerate(quarters):
                ve.tensor_tensor(chunk(0, c), x_all[:, 1 + qs.start:1 + qs.stop, :], bc(ns[:, 1, qs], D, B // 4),
                                 ALU.subtract).then_inc(s_sum, 1)
            dve.wait_ge(s_deg, 1)
            whole(inverse_root(run, degrees[:], ns[:, 3, :], ns[:, 4, :], ns[:, 5, :], ns[:, 6, :], degree_roots[:, 0, :]))
            ve.tensor_tensor(degree_roots[:, 1, :], degree_roots[:, 0, :], degrees[:], ALU.mult)
            for c, qs in enumerate(quarters):
                dve.wait_ge(s_sq, c + 1)
                last = ve.tensor_reduce(ns[:, 0, qs], chunk(1, c), AX_X, ALU.add)
            step(last)
            ve.tensor_scalar(ns[:, 2, :], ns[:, 0, :], 1.0 / D, LN_EPS, ALU.mult, ALU.add).then_inc(s_var, 1)
            dve.wait_ge(s_var, 1)
            dve.wait_ge(s_root, 1)
            whole(inverse_root(run, ns[:, 2, :], ns[:, 3, :], ns[:, 4, :], ns[:, 5, :], ns[:, 6, :], ns[:, 7, :]))
            for c, qs in enumerate(quarters):
                last = ve.scalar_tensor_tensor(out=h2_all[:, qs, :], in0=chunk(0, c), scalar=0.0,
                                               in1=bc(ns[:, 7, qs], D, B // 4), op0=ALU.max, op1=ALU.mult)
            step(last)
            step(ve.tensor_reduce(bn_part[:, 0, :], h2_all[:].rearrange("p b f -> p f b"), AX_X, ALU.add))
            ve.tensor_copy(bn_part[:, 1, :], bn_part[:, 0, :]).then_inc(s_bn, 1)
            dve.wait_ge(s_bnp, 3)
            ve.tensor_scalar(bn_mean_c[:], bank[0][:, 64:65], 1.0 / (B * N), None, ALU.mult)
            ve.tensor_scalar(bn_mean_bc[:], bank[0][:, 0:D], 1.0 / (B * N), None, ALU.mult).then_inc(s_bn, 1)
            dve.wait_ge(s_bn, 2)
            for c, qs in enumerate(quarters):
                ve.tensor_tensor(chunk(0, c), h2_all[:, qs, :],
                                 bn_mean_bc[:].rearrange("p (o f) -> p o f", o=1).broadcast_to([N, B // 4, D]),
                                 ALU.subtract).then_inc(s_sum, 1)
            for c in range(4):
                dve.wait_ge(s_sq, 4 + c + 1)
                last = ve.tensor_reduce(bn_parts[:, c, :], chunk(1, c).rearrange("p b f -> p f b"), AX_X, ALU.add)
            step(last)
            step(ve.tensor_reduce(bn_part[:, 0, :], bn_parts[:].rearrange("p c f -> p f c"), AX_X, ALU.add))
            ve.tensor_copy(bn_part[:, 1, :], bn_part[:, 0, :]).then_inc(s_bn, 1)
            dve.wait_ge(s_bnp, 4)
            ve.tensor_scalar(bn_v[:, 0:1], bank[0][:, 64:65], 1.0 / (B * N), BN_EPS, ALU.mult, ALU.add).then_inc(s_bn, 1)
            dve.wait_ge(s_bna, 1)
            dve.wait_ge(s_bn, 4)
            whole(inverse_root(run, bn_v[:, 0:1], bn_v[:, 1:2], bn_v[:, 2:3], bn_v[:, 3:4], bn_v[:, 4:5], bn_v[:, 5:6]))
            step(ve.tensor_tensor(bn_v[:, 6:7], bn_v[:, 5:6], gamma_c[:], ALU.mult))
            step(ve.tensor_tensor(bn_v[:, 7:8], bn_mean_c[:], bn_v[:, 6:7], ALU.mult))
            step(ve.tensor_tensor(bn_v[:, 0:1], beta_c[:], bn_v[:, 7:8], ALU.subtract))
            for k, half in enumerate((slice(0, D), slice(D, 2 * D))):
                ve.tensor_scalar(ws3_pair[half, k, :], w3[half], bn_v[half, 6:7], None, ALU.mult)
            ve.tensor_copy(shift_bc[:], bn_v[0:D, 0:1].broadcast_to([D, N])).then_inc(s_bn, 1)
            dve.wait_ge(s_bnp, 5)
            ve.tensor_tensor(cb3[:], bank[1][:, 0:D], b3_bc[:], ALU.add).then_inc(s_bn, 1)
            dve.wait_ge(s_bn, 6)

            def aggregate_2(u, t):
                step = piecewise(dve, L_steps[u], V_P2, t)
                st = stat[u]
                dve.wait_ge(s_a2[u], t * 16 + 16)
                yield from step(ve.tensor_scalar(no_edge[u], abuf[u][:], 0.0, NEG_INF, ALU.is_le, ALU.mult))
                yield
                dve.wait_ge(L.sem("at_psum", u), L.now("at_psum", t))
                ve.memset(st[:, 11, :], 0.0).then_inc(L.sem("a_used", u), 1)
                yield from pieces(4)
                dve.wait_ge(L.sem("x_psum", u), L.now("x_psum", t))
                yield from step(ve.tensor_tensor(xl[u], bank[2 * u][:, 0:GB * D].rearrange("p (b f) -> p b f", b=GB),
                                                 cb3[:].rearrange("p (o f) -> p o f", o=1).broadcast_to([N, GB, D]), ALU.add))
                ve.tensor_tensor(yl[u], xl[u], bc(degree_roots[:, 0, bass.ds((t * U + u) * GB, GB)]), ALU.mult)\
                    .then_inc(L.sem("y_ready", u), 1)
                yield from pieces(4)
                dve.wait_ge(L.sem("ay_psum", u), L.now("ay_psum", t))
                yield from step(ve.tensor_tensor(tmp[u][:], bank[2 * u + 1][:, 0:GB * D].rearrange("p (b f) -> p b f", b=GB),
                                                 bc(degree_roots[:, 1, bass.ds((t * U + u) * GB, GB)]), ALU.mult))
                assert step.done[0] == V_AY, step.done

            def residual_norm(u, t):
                yield
                step = piecewise(dve, L_steps[u], V_P2, t, V_AY)
                x = x_all[:, bass.ds((t * U + u) * GB + 1, GB), :]
                yield from step(ve.tensor_tensor(xc[u][:], xl[u], tmp[u][:], ALU.subtract))
                yield from step(ve.scalar_tensor_tensor(out=tmp[u][:], in0=xc[u][:], scalar=LEAK2, in1=xc[u][:],
                                                        op0=ALU.mult, op1=ALU.max))
                yield from step(ve.tensor_tensor(x, x, tmp[u][:], ALU.add))
                yield from variance(step, x, u, t, L, "", 1)
                assert step.done[0] == V_VAR, step.done

            def attention_logits(u, t):
                step = piecewise(dve, L_steps[u], V_P2, t, V_VAR)
                st = stat[u]
                dve.wait_ge(L.sem("v", u), L.now("v", t))
                dve.wait_ge(L.sem("root", u), L.now("root", t))
                yield from newton(step, st[:, 2, :], st[:, 4, :], st[:, 5, :], st[:, 6, :], st[:, 7, :])
                relu_scaled(h2_h3[u], u).then_inc(L.sem("h3_ready", u), 1)
                assert step.done[0] == V_H3, step.done

            def attention_sums(u, t):
                step = piecewise(dve, L_steps[u], V_P2, t, V_H3)
                st = stat[u]
                x = x_all[:, bass.ds((t * U + u) * GB + 1, GB), :]
                dve.wait_ge(L.sem("e_copied", u), L.now("e_copied", t))
                yield from step(ve.scalar_tensor_tensor(out=logits[u], in0=pairs[u], scalar=LEAK3, in1=pairs[u],
                                                        op0=ALU.mult, op1=ALU.max))
                yield from step(ve.tensor_tensor(no_edge[u], logits[u], no_edge[u], ALU.add))
                ve.tensor_reduce(st[:, 9, :], no_edge[u], AX_X, ALU.max, negate=True).then_inc(L.sem("max_ready", u), 1)
                yield from pieces(6)
                dve.wait_ge(L.sem("exp_done", u), L.now("exp_done", t))
                yield from step(ve.reciprocal(st[:, 8, :], st[:, 10, :]))
                dve.wait_ge(L.sem("att_psum", u), L.now("att_psum", t))
                yield from step(ve.tensor_tensor(xl[u], bank[2 * u][:, 0:GB * D].rearrange("p (b f) -> p b f", b=GB),
                                                 bc(st[:, 8, :]), ALU.mult))
                ve.tensor_scalar(tmp[u][:], xl[u], 0.0, None, ALU.min).then_inc(L.sem("att_scaled", u), 1)
                yield from step(ve.scalar_tensor_tensor(out=xc[u][:], in0=xl[u], scalar=0.0, in1=x, op0=ALU.max, op1=ALU.add))
                dve.wait_ge(L.sem("elu_exp", u), L.now("elu_exp", t))
                dve.wait_ge(s_out_free[u], t + 1)
                ve.scalar_tensor_tensor(out=outb[u], in0=yl[u], scalar=-1.0, in1=xc[u][:], op0=ALU.add,
                                        op1=ALU.add).then_inc(L.sem("out_ready", u), 1)
                assert step.done[0] == V_P2, step.done

            stages_in_turn(dve, (aggregate_2, residual_norm, attention_logits, attention_sums))


_INS = ['x', 'adj', 'L1_gnn_W1', 'L1_gnn_b1', 'L1_gnn_W2', 'L1_gnn_b2', 'L2_gnn_gamma', 'L2_gnn_beta',
        'L2_gnn_W', 'L2_gnn_b', 'L3_gnn_W', 'L3_gnn_a']


def kernel(**inputs):
    import numpy as np
    import concourse.bacc as bacc
    from concourse.bass_utils import run_bass_kernel_spmd

    nc = bacc.Bacc("TRN2", target_bir_lowering=False, num_devices=1)
    arrays, args = {}, []
    for name in _INS:
        a = np.ascontiguousarray(inputs[name])
        arrays[f"in_{name}"] = a
        args.append(nc.dram_tensor(f"in_{name}", a.shape, mybir.dt.from_np(a.dtype), kind="ExternalInput").ap())
    out = nc.dram_tensor("out", (B, N, D), F32, kind="ExternalOutput").ap()
    layers(nc, *args, out)
    r = run_bass_kernel_spmd(nc, [arrays], core_ids=[0])
    return r.results[0]["out"]
```
